# Optimizing a Trainium2 kernel written in Bass

```python
import numpy as np
import jax
import jax.numpy as jnp

def _softmax(x, axis=-1):
    return jax.nn.softmax(x, axis=axis)

def _gelu(x):
    return jax.nn.gelu(x, approximate=True)

def _silu(x):
    return jax.nn.silu(x)

def _sigmoid(x):
    return jax.nn.sigmoid(x)

def _layernorm(x, axis=-1, eps=1e-05):
    m = jnp.mean(x, axis=axis, keepdims=True)
    v = jnp.var(x, axis=axis, keepdims=True)
    return (x - m) / jnp.sqrt(v + eps)

def _scatter_add(tgt, idx, src, axis=0):
    return tgt.at[idx].add(src)

def _segment_sum(src, seg, n):
    return jax.ops.segment_sum(src, seg, n)
kernel_name = 'mk_rec_standalone_d1_rec_r8_11a73a'

def setup_inputs(seed: int=0):
    np.random.seed(seed)
    _w = jnp.asarray

    def _rec_inputs():
        import jax
        import jax.numpy as jnp
        _rk = jax.random.key(seed)
        r_x = -0.000611745 + 1.00059 * jax.random.normal(jax.random.fold_in(_rk, 1), (512, 39, 16), jnp.float32)
        return r_x
    r_x = _rec_inputs()

    def _L0_rec_setup():
        import jax, jax.numpy as jnp
        import numpy as np
        F0 = 39
        CIN_SIZES = [128, 128, 128]
        B, D = (512, 16)

        def _cin_forward(x, weights, biases):
            x0 = x
            xk = x
            fields = [F0] + CIN_SIZES
            outs = []
            for idx, s in enumerate(CIN_SIZES):
                fk = fields[idx]
                w = weights[idx].reshape(F0, fk, s)
                out = jnp.einsum('bid,bjd,ijs->bsd', x0, xk, w) + biases[idx][None, :, None]
                outs.append(out)
                xk = out
            res = jnp.concatenate(outs[1:], axis=1)
            return jnp.sum(res, axis=-1)
        key = jax.random.key(seed)
        ks = jax.random.split(key, 7)
        fields = [F0] + CIN_SIZES
        inp = {'x': jax.random.normal(ks[0], (B, F0, D), dtype=jnp.float32)}
        for i, s in enumerate(CIN_SIZES):
            m = fields[i] * F0
            inp[f'w{i}'] = jax.random.normal(ks[1 + 2 * i], (m, s), dtype=jnp.float32) * (2.0 / (m + s)) ** 0.5
            inp[f'b{i}'] = jax.random.normal(ks[2 + 2 * i], (s,), dtype=jnp.float32) * 0.02
        return inp
    _L0_rec_all = _L0_rec_setup()
    _L0_rec_in = {k: v for k, v in _L0_rec_all.items() if k in ('w0', 'b0', 'w1', 'b1', 'w2', 'b2')}
    del _L0_rec_all
    return {'r_x': r_x, 'L0_rec_w0': _L0_rec_in['w0'], 'L0_rec_b0': _L0_rec_in['b0'], 'L0_rec_w1': _L0_rec_in['w1'], 'L0_rec_b1': _L0_rec_in['b1'], 'L0_rec_w2': _L0_rec_in['w2'], 'L0_rec_b2': _L0_rec_in['b2']}

def reference(r_x, L0_rec_w0, L0_rec_b0, L0_rec_w1, L0_rec_b1, L0_rec_w2, L0_rec_b2):
    import jax
    import jax.numpy as jnp

    def _L0_rec_ref(x, w0, b0, w1, b1, w2, b2):
        import jax, jax.numpy as jnp
        import numpy as np
        F0 = 39
        CIN_SIZES = [128, 128, 128]
        B, D = (512, 16)

        def _cin_forward(x, weights, biases):
            x0 = x
            xk = x
            fields = [F0] + CIN_SIZES
            outs = []
            for idx, s in enumerate(CIN_SIZES):
                fk = fields[idx]
                w = weights[idx].reshape(F0, fk, s)
                out = jnp.einsum('bid,bjd,ijs->bsd', x0, xk, w) + biases[idx][None, :, None]
                outs.append(out)
                xk = out
            res = jnp.concatenate(outs[1:], axis=1)
            return jnp.sum(res, axis=-1)
        return _cin_forward(x, [w0, w1, w2], [b0, b1, b2])
    y = _L0_rec_ref(r_x, L0_rec_w0, L0_rec_b0, L0_rec_w1, L0_rec_b1, L0_rec_w2, L0_rec_b2)
    return y

_drawn_inputs = setup_inputs


def setup_inputs(seed=0):
    import zlib

    import numpy as np

    out = dict(_drawn_inputs(seed))
    spreads = {}
    factors = {'L0_rec_b0': 3.951}
    for name, (base, spread) in spreads.items():
        noise = np.random.default_rng([zlib.crc32(name.encode()), seed]).standard_normal(out[name].shape)
        drawn = base * np.exp(spread * noise) if base else spread * noise
        out[name] = jnp.asarray(drawn.astype(out[name].dtype))
    for name, factor in factors.items():
        out[name] = (out[name] * factor).astype(out[name].dtype)
    return out
```

```python
import concourse.bass as bass
from concourse import mybir
from contextlib import ExitStack


B, F, D, S = 512, 39, 16, 128
P = 128
N = B * D
NT = N // P
TG = 4
NG = NT // TG
GN = TG * P
BT = P // D
BG = TG * BT
SHIFTS = F // 2 + 1
SC = P // F
NCH = -(-SHIFTS // SC)
ROWS = [F * min(SC, SHIFTS - SC * c) for c in range(NCH)]
R = F * SC
QI = 4
NQ = -(-F // QI)
WIDE = [min(QI, F - QI * k) for k in range(NQ)]
NV = (NQ + 1) // 2
NS = NQ // 2
VOPS = sum(WIDE[0::2])
GQ = TG * NQ
GC = F + 1
RING = 3
PG = 2
FOLD = 5
ADDS = NS - 1
L0_AT = [4 * c + 5 for c in range(NCH)]
G_AT = 8


def build(nc, xt2, xn, w0p, w0q, w1, w2, b0, b1, b2, mask, ident, out):
    f32 = mybir.dt.float32
    f32r = mybir.dt.float32r
    ALU = mybir.AluOpType
    ACT = mybir.ActivationFunctionType

    ctx = ExitStack()
    with ctx:
        def sb(name, shape, dt=f32):
            return ctx.enter_context(nc.sbuf_tensor(name, shape, dt))

        def pb(name):
            return ctx.enter_context(nc.psum_tensor(name, [P, 512], f32))

        def sem(name):
            return ctx.enter_context(nc.semaphore(name))

        w0s = sb("w0s", [R, NCH, S])
        w1h = sb("w1h", [P, F * S], f32r)
        w1l = sb("w1l", [P, F * S], f32r)
        xa = [sb(f"xa{p}", [R, GN]) for p in range(2)]
        xb = sb("xb", [P, 2, NCH, GN])
        xg = [sb(f"xg{p}", [P, TG, F]) for p in range(2)]
        xs = [sb(f"xs{p}", [P, TG, 2, F]) for p in range(2)]
        z = [sb(f"z{p}", [R, GN]) for p in range(2)]
        h0h = [sb(f"h0h{p}", [P, GN], f32r) for p in range(2)]
        h0l = [sb(f"h0l{p}", [P, GN], f32r) for p in range(2)]
        acc = [sb(f"acc{p}", [P, QI * S]) for p in range(2)]
        prod = sb("prod", [P, NS, QI * S])
        psum_q = [sb(f"sumq{p}", [P, QI * S]) for p in range(2)]
        h1 = sb("h1", [P, S])
        h1h = sb("h1h", [P, S], f32r)
        h1l = sb("h1l", [P, S], f32r)
        xblk = [sb(f"xblk{p}", [P, 2, GC, BT], f32r) for p in range(2)]
        gg = [sb(f"gg{p}", [P, GC, BG]) for p in range(2)]
        G = sb("G", [P, NG, GC, BG])
        b0c = sb("b0c", [P, 1])
        b2c = sb("b2c", [P, 1])
        b2d = sb("b2d", [P, 1])
        b1r = sb("b1r", [P, S])
        msk = sb("msk", [P, BT])
        idn = sb("idn", [P, P])
        one = sb("one", [P, 1])
        STG = -(-F * S // (GC * BG))
        w1f = G[:, NG - STG:NG, :, :].rearrange("p g c b -> p (g c b)")[:, 0:F * S]
        w0a = G[0:R, 0:1, :, :].rearrange("p g c b -> p (g c b)")[:, 0:NCH * S].rearrange("p (c s) -> p c s", c=NCH)
        w0b = G[0:R, 1:2, :, :].rearrange("p g c b -> p (g c b)")[:, 0:NCH * S].rearrange("p (c s) -> p c s", c=NCH)
        y2s, y1s = acc
        osb = prod

        bankv = [pb(f"bankv{n}") for n in range(RING)]
        banks = [pb(f"banks{n}") for n in range(RING)]
        bankh = pb("bankh")
        bankg = pb("bankg")

        s_const = sem("const_loaded")
        s_w0in = sem("w0_loaded")
        s_w1in = [sem(f"w1_loaded{n}") for n in range(2)]
        s_w2in = sem("w2_loaded")
        s_x = [sem(f"x_loaded{p}") for p in range(2)]
        s_xp = [sem(f"x_pairs_loaded{p}") for p in range(2)]
        s_w0 = sem("w0_summed")
        s_w1h = sem("w1_rounded")
        s_w1l = sem("w1_split")
        s_b2 = sem("b2_scaled")
        s_z = sem("pairs_ready")
        s_l0 = sem("pairs_used")
        s_h0h = sem("h0_rounded")
        s_h0l = sem("h0_split")
        s_t = sem("quad_ready")
        s_v = sem("quad_summed")
        s_s = sem("quad_multiplied")
        s_q = sem("products_summed")
        s_f = sem("tile_folded")
        s_xs = sem("x_split")
        s_xk = sem("blocks_ready")
        s_mk = sem("blocks_cleared")
        s_g = sem("g_ready")
        s_ge = sem("g_copied")
        s_gs = [sem(f"g_stored{p}") for p in range(2)]
        s_y = sem("y2_ready")
        s_yc = sem("y2_copied")
        s_yt = sem("y_turned")
        s_yo = sem("y_copied")
        s_out = sem("y_stored")

        w2v = xb[:, :, :, :].rearrange("p a c n -> p (a c n)")[:, 0:F * S]

        block = ctx.enter_context(nc.Block())

        def bodies(eng, body):
            body(0, True, False)
            with eng.Fori(1, NG // PG - 1) as r:
                body(r, False, False)
            body(NG // PG - 1, False, True)

        @block.sync
        def _(sp):
            def load_pairs(col, p):
                x0 = xt2[0:F, bass.ds(col, GN)]
                for s in range(SC):
                    sp.dma_start(xa[p][s * F:(s + 1) * F, :], x0).then_inc(s_xp[p], 16)
                    n = NCH if SC * (NCH - 1) + s < SHIFTS else NCH - 1
                    sp.dma_start(xb[s * F:(s + 1) * F, p, 0:n, :],
                                 bass.AP(x0.tensor, x0.offset + s * N, [[N, F], [SC * N, n], [1, GN]])
                                 ).then_inc(s_xp[p], 16)

            def load_columns(tile, p):
                sp.dma_start(xg[p][:, :, :], xn[:, bass.ds(tile, TG), :]).then_inc(s_x[p], 16)

            for p in range(PG):
                load_pairs(p * GN, p)
                load_columns(p * TG, p)

            def body(r, first, last):
                for p in range(PG):
                    g = r * PG + p
                    col, tile, before = (v if isinstance(v, int) else sp.snap(v)
                                         for v in ((g + 2) * GN, (g + 1) * TG, g - 1))
                    if not last:
                        sp.wait_ge(s_z, (g + 1) * NCH)
                        load_pairs(col, p)
                    elif p == 0:
                        sp.wait_ge(s_z, NG * NCH)
                        sp.dma_start(w2v, w2).then_inc(s_w2in, 16)
                    if first and p == 0:
                        continue
                    if first:
                        sp.wait_ge(s_w1l, NQ)
                        sp.wait_ge(s_w1h, NQ)
                        sp.wait_ge(s_w0, 1)
                    sp.wait_ge(s_ge, g * TG)
                    sp.dma_start(G[:, bass.ds(before, 1), :, :], gg[1 - p][:, :, :]).then_inc(s_gs[1 - p], 16)
                    if not (last and p == PG - 1):
                        load_columns(tile, 1 - p)

            bodies(sp, body)
            sp.wait_ge(s_ge, NT)
            sp.dma_start(G[:, NG - 1:NG, :, :], gg[(NG - 1) % 2][:, :, :]).then_inc(s_gs[(NG - 1) % 2], 16)
            for bt in range(B // P):
                sp.wait_ge(s_yo, bt + 1)
                sp.dma_start(out[bt * P:(bt + 1) * P, :], osb[:, bt, 0:2 * S]).then_inc(s_out, 16)
            sp.wait_ge(s_out, 16 * (B // P))

        @block.scalar
        def _(act):
            act.dma_start(w0a, w0p).then_inc(s_w0in, 16)
            act.dma_start(w0b, w0q).then_inc(s_w0in, 16)
            half = F * S // 2 // 512 * 512
            act.dma_start(w1f[:, 0:half], w1[:, 0:half]).then_inc(s_w1in[0], 16)
            act.dma_start(b0c[:, :], b0).then_inc(s_const, 16)
            act.dma_start(b2c[:, :], b2).then_inc(s_const, 16)
            act.dma_start(b1r[:, :], b1.partition_broadcast(P)).then_inc(s_const, 16)
            act.dma_start(msk[:, :], mask).then_inc(s_const, 16)
            act.dma_start(idn[:, :], ident).then_inc(s_const, 16)
            act.dma_start(w1f[:, half:F * S], w1[:, half:F * S]).then_inc(s_w1in[1], 16)

            def round_h0(g, p):
                act.wait_ge(s_l0, (g + 1) * NCH)
                nc.scalar.activation(h0h[p][:, :], bankh[:, :], ACT.Identity,
                                     bias=b0c[:, 0:1]).then_inc(s_h0h, 1)

            def copy_g(t, q, p):
                act.wait_ge(s_g, t + 1)
                nc.scalar.activation(gg[p][:, :, q * BT:(q + 1) * BT],
                                     bankg[:, 0:GC * BT].rearrange("p (c b) -> p c b", b=BT),
                                     ACT.Copy).then_inc(s_ge, 1)

            act.wait_ge(s_const, 16 * 5)
            nc.scalar.mul(b2d[:, :], b2c[:, :], float(D)).then_inc(s_b2, 1)
            round_h0(0, 0)
            for k in range(NQ):
                lo, hi = QI * S * k, QI * S * k + S * WIDE[k]
                act.wait_ge(s_w1in[hi > half], 16)
                nc.scalar.activation(w1h[:, lo:hi], w1f[:, lo:hi], ACT.Copy).then_inc(s_w1h, 1)

            def body(r, first, last):
                for p in range(PG):
                    g = r * PG + p
                    act.wait_ge(s_x[p], (r + 1) * 16)
                    for q in range(TG):
                        t = g * TG + q
                        ti = p * TG + q
                        for n in range(NS):
                            k = 2 * n + 1
                            act.wait_ge(s_t, g * GQ + (q * NQ + k + 1))
                            if not (first and ti == 0):
                                act.wait_ge(s_q, t * ADDS + (max(n, 1) - ADDS))
                            bank = banks[n % RING]
                            for m in range(WIDE[k]):
                                i = QI * k + m
                                a = nc.scalar.activation(prod[:, n, m * S:(m + 1) * S],
                                                         bank[:, m * S:(m + 1) * S], ACT.Copy,
                                                         scale=xg[p][:, q, i:i + 1])
                            a.then_inc(s_s, 1)
                            if q == TG - 1 and n == 0 and not (last and p == PG - 1):
                                round_h0(g + 1, 1 - p)
                        if not (first and ti == 0):
                            pt = p if q else 1 - p
                            if q == 1 and not (first):
                                act.wait_ge(s_gs[p], r * 16)
                            copy_g(t - 1, (q - 1) % TG, pt)

            bodies(act, body)
            copy_g(NT - 1, TG - 1, (NG - 1) % 2)
            act.wait_ge(s_gs[0], 16 * (NG // 2))
            act.wait_ge(s_gs[1], 16 * (NG // 2))
            nc.scalar.activation(y1s[:, :].rearrange("p (g b) -> p g b", b=BG), G[:, :, F, :],
                                 ACT.Copy).then_inc(s_yc, 1)
            act.wait_ge(s_y, 1)
            act.wait_ge(s_b2, 1)
            nc.scalar.activation(y2s[:, :], bankh[:, :], ACT.Identity, bias=b2d[:, 0:1]).then_inc(s_yc, 1)

        @block.vector
        def _(dve):
            def pairs(g, c, p):
                nc.vector.tensor_tensor(z[c % 2][0:ROWS[c], :], xa[p][0:ROWS[c], :],
                                        xb[0:ROWS[c], p, c, :], ALU.mult).then_inc(s_z, 1)

            def split_h0(g, p):
                dve.wait_ge(s_h0h, g + 1)
                nc.vector.scalar_tensor_tensor(out=h0l[p][:, :], in0=bankh[:, :], scalar=b0c[:, 0:1],
                                               in1=h0h[p][:, :].bitcast(f32), op0=ALU.add,
                                               op1=ALU.subtract).then_inc(s_h0l, 1)

            def fold(t, a):
                dve.wait_ge(s_q, (t + 1) * ADDS)
                dve.wait_ge(s_v, (t + 1) * VOPS)
                s4 = acc[a]
                nc.vector.tensor_tensor(s4[:, :], s4[:, :], psum_q[a][:, :], ALU.add).then_inc(s_f, 1)
                dve.wait_ge(s_f, t * FOLD + 1)
                nc.vector.tensor_tensor(s4[:, 0:2 * S], s4[:, 0:2 * S], s4[:, 2 * S:4 * S],
                                        ALU.add).then_inc(s_f, 1)
                dve.wait_ge(s_f, t * FOLD + 2)
                nc.vector.tensor_tensor(h1[:, :], s4[:, 0:S], s4[:, S:2 * S], ALU.add).then_inc(s_f, 1)
                dve.wait_ge(s_f, t * FOLD + 3)
                if not (isinstance(t, int) and t == 0):
                    dve.wait_ge(s_g, t)
                nc.vector.tensor_copy(h1h[:, :], h1[:, :]).then_inc(s_f, 1)
                dve.wait_ge(s_f, t * FOLD + 4)
                nc.vector.tensor_tensor(h1l[:, :], h1[:, :], h1h[:, :].bitcast(f32),
                                        ALU.subtract).then_inc(s_f, 1)

            dve.wait_ge(s_w0in, 32)
            nc.vector.tensor_tensor(w0s[:, :, :], w0a, w0b, ALU.add).then_inc(s_w0, 1)
            dve.wait_ge(s_xp[0], 16 * 2 * SC)
            for c in range(NCH):
                if c >= 2:
                    dve.wait_ge(s_l0, c - 1)
                pairs(0, c, 0)
            dve.wait_ge(s_const, 16 * 5)
            split_h0(0, 0)
            for k in range(NQ):
                lo, hi = QI * S * k, QI * S * k + S * WIDE[k]
                dve.wait_ge(s_w1h, k + 1)
                nc.vector.tensor_tensor(w1l[:, lo:hi], w1f[:, lo:hi], w1h[:, lo:hi].bitcast(f32),
                                        ALU.subtract).then_inc(s_w1l, 1)

            def body(r, first, last):
                for p in range(PG):
                    g = r * PG + p
                    dve.wait_ge(s_x[p], (r + 1) * 16)
                    for q in range(TG):
                        t = g * TG + q
                        ti = p * TG + q
                        a = ti % 2
                        done = 0
                        for n in range(NV):
                            k = 2 * n
                            dve.wait_ge(s_t, g * GQ + (q * NQ + k + 1))
                            bank = bankv[n % RING]
                            for m in range(WIDE[k]):
                                i = QI * k + m
                                part = acc[a][:, m * S:(m + 1) * S]
                                tq = bank[:, m * S:(m + 1) * S]
                                x = xg[p][:, q, i:i + 1]
                                if n == 0 and m == 0:
                                    ins = nc.vector.scalar_tensor_tensor(out=part, in0=tq, scalar=x, in1=b1r[:, :],
                                                                         op0=ALU.mult, op1=ALU.add)
                                elif n == 0:
                                    ins = nc.vector.tensor_scalar(part, tq, x, None, ALU.mult)
                                else:
                                    dve.wait_ge(s_v, t * VOPS + (done - QI + 1))
                                    ins = nc.vector.scalar_tensor_tensor(out=part, in0=tq, scalar=x, in1=part,
                                                                         op0=ALU.mult, op1=ALU.add)
                                ins.then_inc(s_v, 1)
                                done += 1
                            v = q * NV + n
                            if not (last and p == PG - 1):
                                if v % 2 == 0 and v // 2 < NCH:
                                    c = v // 2
                                    if c == 0:
                                        if p == 0:
                                            dve.wait_ge(s_xp[1], (r + 1) * 16 * 2 * SC)
                                        else:
                                            dve.wait_ge(s_xp[0], (r + 2) * 16 * 2 * SC)
                                    dve.wait_ge(s_l0, (g + 1) * NCH + (c - 1 if c >= 2 else 0))
                                    pairs(g + 1, c, 1 - p)
                                if v == 16:
                                    split_h0(g + 1, 1 - p)
                            if n == 2 and not (first and ti == 0):
                                fold(t - 1, 1 - a)

            bodies(dve, body)
            fold(NT - 1, (NT - 1) % 2)
            for bt in range(B // P):
                dve.wait_ge(s_yt, bt + 1)
                nc.vector.tensor_copy(osb[:, bt, 0:2 * S], bankv[bt % 2][:, 0:2 * S]).then_inc(s_yo, 1)

        @block.gpsimd
        def _(pool):
            for p in range(2):
                nc.gpsimd.memset(xblk[p][:, :, :, :].bitcast(f32), 0.0).then_inc(s_mk, 1)
            nc.gpsimd.memset(one[:, :], 1.0).then_inc(s_mk, 1)
            pool.wait_ge(s_mk, 3)
            pool.wait_ge(s_const, 16 * 5)
            for p in range(2):
                nc.gpsimd.tensor_copy(xblk[p][:, 0, F, :], msk[:, :]).then_inc(s_mk, 1)

            def blocks(t, q, p, a):
                nc.gpsimd.tensor_tensor(
                    xblk[a][:, :, 0:F, :], xs[p][:, q, :, :].unsqueeze(3).broadcast_to([P, 2, F, BT]),
                    msk[:, :].unsqueeze(1).unsqueeze(1).broadcast_to([P, 2, F, BT]), ALU.mult).then_inc(s_xk, 1)

            def body(r, first, last):
                for p in range(PG):
                    g = r * PG + p
                    pool.wait_ge(s_x[p], (r + 1) * 16)
                    nc.gpsimd.tensor_tensor(xs[p][:, :, 0, :].bitcast(f32r), xg[p][:, :, :],
                                            one[:, :].unsqueeze(2).broadcast_to([P, TG, F]),
                                            ALU.mult).then_inc(s_xs, 1)
                    pool.wait_ge(s_xs, 2 * g + 1)
                    nc.gpsimd.tensor_tensor(xs[p][:, :, 1, :], xg[p][:, :, :], xs[p][:, :, 0, :],
                                            ALU.subtract).then_inc(s_xs, 1)
                    for q in range(TG):
                        t = g * TG + q
                        ti = p * TG + q
                        a = ti % 2
                        for n in range(1, NS):
                            w = S * WIDE[2 * n + 1]
                            pool.wait_ge(s_s, t * NS + (n + 1))
                            if n == 1:
                                if not (first and ti < 2):
                                    pool.wait_ge(s_f, t * FOLD + (1 - 2 * FOLD))
                                nc.gpsimd.tensor_tensor(psum_q[a][:, :], prod[:, 0, :], prod[:, 1, :],
                                                        ALU.add).then_inc(s_q, 1)
                            else:
                                pool.wait_ge(s_q, t * ADDS + (n - 1))
                                nc.gpsimd.tensor_tensor(psum_q[a][:, 0:w], psum_q[a][:, 0:w], prod[:, n, 0:w],
                                                        ALU.add).then_inc(s_q, 1)
                            if n == 2:
                                if q == 0:
                                    pool.wait_ge(s_xs, 2 * g + 2)
                                if first and ti < 2:
                                    pool.wait_ge(s_mk, 5)
                                else:
                                    pool.wait_ge(s_g, t - 1)
                                blocks(t, q, p, a)

            bodies(pool, body)

        @block.tensor
        def _(pe):
            def layer0(g, c):
                pe.wait_ge(s_z, g * NCH + (c + 1))
                nc.tensor.matmul(bankh[:, :], w0s[0:ROWS[c], c, :], z[c % 2][0:ROWS[c], :],
                                 start=(c == 0), stop=(c == NCH - 1)).then_inc(s_l0, 1)

            def into_g(t, a):
                pe.wait_ge(s_f, (t + 1) * FOLD)
                pe.wait_ge(s_xk, t + 1)
                if not (isinstance(t, int) and t == 0):
                    pe.wait_ge(s_ge, t)
                def xk(half):
                    return xblk[a][:, half, :, :].rearrange("p c b -> p (c b)")
                o = bankg[:, 0:GC * BT]
                nc.tensor.matmul(o, h1h[:, :], xk(0), start=True, stop=False)
                nc.tensor.matmul(o, h1h[:, :], xk(1), start=False, stop=False)
                nc.tensor.matmul(o, h1l[:, :], xk(0), start=False, stop=True).then_inc(s_g, 1)

            pe.wait_ge(s_w0, 1)
            for c in range(NCH):
                layer0(0, c)

            def body(r, first, last):
                for p in range(PG):
                    g = r * PG + p
                    for q in range(TG):
                        t = g * TG + q
                        ti = p * TG + q
                        for k in range(NQ):
                            w = S * WIDE[k]
                            n = k // 2
                            if q == 0 and k == 0:
                                pe.wait_ge(s_h0l, g + 1)
                            if first and ti == 0:
                                pe.wait_ge(s_w1l, k + 1)
                            if k % 2 == 0:
                                if n >= RING:
                                    pe.wait_ge(s_v, t * VOPS + sum(WIDE[0:k - 2 * RING + 1:2]))
                                elif not (first and ti == 0):
                                    last_n = n + RING if n + RING < NV else n
                                    pe.wait_ge(s_v, t * VOPS + (sum(WIDE[0:2 * last_n + 1:2]) - VOPS))
                                bank = bankv[n % RING]
                            else:
                                if n >= RING:
                                    pe.wait_ge(s_s, t * NS + (n - RING + 1))
                                elif not (first and ti == 0):
                                    last_n = n + RING if n + RING < NS else n
                                    pe.wait_ge(s_s, t * NS + (last_n + 1 - NS))
                                bank = banks[n % RING]
                            c0 = QI * S * k
                            hh, hl = h0h[p][:, q * P:(q + 1) * P], h0l[p][:, q * P:(q + 1) * P]
                            nc.tensor.matmul(bank[:, 0:w], hh, w1h[:, c0:c0 + w], start=True, stop=False)
                            nc.tensor.matmul(bank[:, 0:w], hh, w1l[:, c0:c0 + w], start=False, stop=False)
                            nc.tensor.matmul(bank[:, 0:w], hl, w1h[:, c0:c0 + w], start=False,
                                             stop=True).then_inc(s_t, 1)
                            u = q * NQ + k
                            if u in L0_AT and not (last and p == PG - 1):
                                c = L0_AT.index(u)
                                if c == 0:
                                    pe.wait_ge(s_h0l, g + 1)
                                layer0(g + 1, c)
                            if k == G_AT and not (first and ti == 0):
                                into_g(t - 1, (ti - 1) % 2)

            bodies(pe, body)
            into_g(NT - 1, (NT - 1) % 2)
            pe.wait_ge(s_gs[0], 16 * (NG // 2))
            pe.wait_ge(s_gs[1], 16 * (NG // 2))
            pe.wait_ge(s_w2in, 16)
            for i in range(F):
                mm = nc.tensor.matmul(bankh[:, :], w2v[:, i * S:(i + 1) * S], G[:, :, i, :],
                                      start=(i == 0), stop=(i == F - 1))
            mm.then_inc(s_y, 1)
            for bt in range(B // P):
                if bt >= 2:
                    pe.wait_ge(s_yo, bt - 1)
                if bt == 0:
                    pe.wait_ge(s_yc, 2)
                nc.tensor.transpose(bankv[bt % 2][:, 0:S], y1s[:, bt * P:(bt + 1) * P], idn[:, :])
                nc.tensor.transpose(bankv[bt % 2][:, S:2 * S], y2s[:, bt * P:(bt + 1) * P],
                                    idn[:, :]).then_inc(s_yt, 1)


def kernel(r_x, L0_rec_w0, L0_rec_b0, L0_rec_w1, L0_rec_b1, L0_rec_w2, L0_rec_b2):
    import numpy as np
    import concourse.bacc as bacc
    from concourse.bass_utils import run_bass_kernel_spmd

    x = np.asarray(r_x)
    xt = x.transpose(1, 0, 2).reshape(F, N)
    w0 = np.asarray(L0_rec_w0).reshape(F, F, S)
    w0p = np.zeros((R, NCH, S), w0.dtype)
    w0q = np.zeros((R, NCH, S), w0.dtype)
    i = np.arange(F)
    for k in range(SHIFTS):
        c, r = divmod(k, SC)
        w0p[r * F:(r + 1) * F, c] = w0[i, (i + k) % F]
        if k:
            w0q[r * F:(r + 1) * F, c] = w0[(i + k) % F, i]
    arrays = {
        "xt2": np.concatenate([xt, xt[:SC * NCH]], axis=0),
        "xn": x.reshape(NT, BT, F, D).transpose(1, 3, 0, 2).reshape(P, NT, F),
        "w0p": w0p,
        "w0q": w0q,
        "w1": np.asarray(L0_rec_w1).reshape(F, S, S).transpose(1, 0, 2).reshape(S, F * S),
        "w2": np.asarray(L0_rec_w2).reshape(F, S, S).transpose(1, 0, 2).reshape(S, F * S),
        "b0": np.asarray(L0_rec_b0).reshape(S, 1),
        "b1": np.asarray(L0_rec_b1).reshape(S),
        "b2": np.asarray(L0_rec_b2).reshape(S, 1),
        "mask": np.kron(np.eye(BT, dtype=np.float32), np.ones((D, 1), np.float32)),
        "ident": np.eye(P, dtype=np.float32),
    }
    nc = bacc.Bacc("TRN2", target_bir_lowering=False, num_devices=1)
    ins, args = {}, []
    for name, a in arrays.items():
        ins[f"in_{name}"] = np.ascontiguousarray(a)
        args.append(nc.dram_tensor(f"in_{name}", a.shape, mybir.dt.from_np(a.dtype), kind="ExternalInput").ap())
    args.append(nc.dram_tensor("out_y", (B, 2 * S), mybir.dt.float32, kind="ExternalOutput").ap())
    build(nc, *args)
    r = run_bass_kernel_spmd(nc, [ins], core_ids=[0])
    return r.results[0]["out_y"]
```

```python
import concourse.bass as bass
from concourse import mybir
from contextlib import ExitStack


B, F, D, S = 512, 39, 16, 128
P = 128
N = B * D
NT = N // P
TG = 4
NG = NT // TG
GN = TG * P
BT = P // D
BG = TG * BT
PG = 2

SHIFTS = F // 2 + 1
SC = P // F
NCH = -(-SHIFTS // SC)
ROWS = [F * min(SC, SHIFTS - SC * c) for c in range(NCH)]
R = F * SC
XB = [(0, 4), (4, NCH)]

QI = 4
NQ = -(-F // QI)
WIDE = [min(QI, F - QI * k) for k in range(NQ)]
GQ = TG * NQ
VQ = [1, 4, 6, 8]
SQ = [0, 2, 3, 5, 7, 9]
NV, NS = len(VQ), len(SQ)
VOPS = QI * NV
ACC, SUM, RAW = 0, QI, 2 * QI
BIAS = RAW + WIDE[SQ[-1]]
SLOTS = BIAS + 1
ADDS = NS - 3
FOLD = 3
GC = F + 1
RING = 3
VBODY, SBODY = NV * TG * PG, NS * TG * PG

PAIRS_U, ROUND_U, SPLIT_U, LAYER0_U, SPACE = -3, 0, 1, 9, 4


def chunk_steps(u0):
    return {(u0 + SPACE * c) % GQ: (c, 1 if u0 + SPACE * c >= 0 else 2) for c in range(NCH)}


def early(u0):
    return [c for c in range(NCH) if u0 + SPACE * c < 0]


H0_ROUND_AT, H0_SPLIT_AT = 34, 35
FOLD_AT = [3, 7, 8]
INTO_G_AT = 3
COPY_G_AT = 6
BLOCKS_AT = 1
SUM_AT = [4, 5, 8]

HB = B // 2
HG = NG // 2
W2S = NCH * GN // 512
GR = 8
LATE = [1, 12]
LATE_COPY = [4, 15]
LATE_FOLD = [1, 3, 5]
W2_ROUND_AT = {4: 0, 8: 1, 9: 2}
W2_SPLIT_AT = {9: 0}


def last_use(index, ring, body):
    bank = index % ring
    same = [j for j in range(index) if j % ring == bank]
    return same[-1] if same else max(j for j in range(body) if j % ring == bank) - body


def build(nc, xt2, xn, w0p, w0q, w1, w2, b0, b1, b2, mask, ident, out):
    f32 = mybir.dt.float32
    f32r = mybir.dt.float32r
    ALU = mybir.AluOpType
    ACT = mybir.ActivationFunctionType
    AX = mybir.AxisListType

    ctx = ExitStack()
    with ctx:
        def sb(name, shape, dt=f32):
            return ctx.enter_context(nc.sbuf_tensor(name, shape, dt))

        def pb(name):
            return ctx.enter_context(nc.psum_tensor(name, [P, 512], f32))

        def sem(name):
            return ctx.enter_context(nc.semaphore(name))

        w0h = sb("w0h", [R, NCH, S], f32r)
        w0l = sb("w0l", [R, NCH, S], f32r)
        wh = sb("wh", [P, F * S], f32r)
        wl = sb("wl", [P, F * S], f32r)
        xa = [sb(f"xa{p}", [R, GN]) for p in range(2)]
        xb = sb("xb", [P, NCH, GN])
        xg = [sb(f"xg{p}", [P, TG, F]) for p in range(2)]
        xs = [sb(f"xs{p}", [P, TG, 2, F]) for p in range(2)]
        zf = [sb(f"zf{p}", [R, GN]) for p in range(2)]
        zh = [sb(f"zh{p}", [P, GN], f32r) for p in range(2)]
        zl = [sb(f"zl{p}", [P, GN], f32r) for p in range(2)]
        h0h = [sb(f"h0h{p}", [P, GN], f32r) for p in range(2)]
        h0l = [sb(f"h0l{p}", [P, GN], f32r) for p in range(2)]
        prod = sb("prod", [P, NS - 1, QI * S])
        slots = [sb(f"slots{p}", [P, SLOTS, S]) for p in range(2)]
        h1 = sb("h1", [P, S])
        h1h = sb("h1h", [P, S], f32r)
        h1l = sb("h1l", [P, S], f32r)
        xblk = [sb(f"xblk{p}", [P, 2, GC, BT], f32r) for p in range(2)]
        gg = [sb(f"gg{p}", [P, GC, BG]) for p in range(2)]
        G = sb("G", [P, NG, GC, BG])
        b0c = sb("b0c", [P, 1])
        b2c = sb("b2c", [P, 1])
        b2d = sb("b2d", [P, 1])
        msk = sb("msk", [P, BT])
        idn = sb("idn", [P, P])
        one = sb("one", [P, 1])

        def staged(rows, g, n):
            return G[0:rows, g:g - (-n // (GC * BG)), :, :].rearrange("p g c b -> p (g c b)")[:, 0:n]

        w0a, w0b, w0f = (staged(R, g, NCH * S).rearrange("p (c s) -> p c s", c=NCH) for g in range(3))
        w1f = staged(P, NG + (-F * S // (GC * BG)), F * S)
        w2f = xb[:, :, :].rearrange("p c n -> p (c n)")
        y1s, y2s = (s[:, :, :].rearrange("p c s -> p (c s)")[:, 0:B] for s in slots)
        osb = prod
        gh = [b[:, n * HB:(n + 1) * HB] for b in (h0h[0], *zh, h0h[1]) for n in range(2)]
        gl = [b[:, n * HB:(n + 1) * HB] for b in (h0l[0], *zl, h0l[1]) for n in range(2)]

        bankv = [pb(f"bankv{n}") for n in range(RING)]
        banks = [pb(f"banks{n}") for n in range(RING)]
        bankh = pb("bankh")
        bankg = pb("bankg")

        s_const = sem("const_loaded")
        s_w0in = sem("w0_loaded")
        s_w1in = [sem(f"w1_loaded{k}") for k in range(0, NQ, 2)]
        s_w2in = [sem(f"w2_loaded{n}") for n in range(2)]
        s_x = [sem(f"x_loaded{p}") for p in range(2)]
        s_xp = [sem(f"x_pairs_loaded{n}") for n in range(len(XB))]
        s_w0 = sem("w0_split")
        s_wh = sem("w_rounded")
        s_wl = sem("w_split")
        s_wv = sem("w2_rounded_by_vector")
        s_b2 = sem("b2_scaled")
        s_z = sem("pairs_made")
        s_zh = sem("pairs_rounded")
        s_zl = sem("pairs_split")
        s_l0 = sem("pairs_used")
        s_h0h = sem("h0_rounded")
        s_h0l = sem("h0_split")
        s_t = sem("quad_ready")
        s_v = sem("products_added")
        s_s = sem("quad_multiplied")
        s_q = sem("products_summed")
        s_f = sem("tile_folded")
        s_xs = sem("x_split")
        s_xk = sem("blocks_ready")
        s_mk = sem("constants_ready")
        s_g = sem("g_ready")
        s_ge = sem("g_copied")
        s_gs = [sem(f"g_stored{p}") for p in range(2)]
        s_gh = sem("g_rounded")
        s_gl = sem("g_split")
        s_gp = sem("g_split_by_gpsimd")
        s_gu = sem("g_used")
        s_yc = sem("y_halves_copied")
        s_yt = sem("y_turned")
        s_yo = sem("y_copied")
        s_out = sem("y_stored")

        block = ctx.enter_context(nc.Block())

        def bodies(eng, body):
            body(0, True, False)
            with eng.Fori(1, NG // PG - 1) as r:
                body(r, False, False)
            body(NG // PG - 1, False, True)

        def turns(r):
            for p in range(PG):
                for q in range(TG):
                    g = r * PG + p
                    yield g, p, q, g * TG + q, p * TG + q

        def columns(k):
            return slice(QI * S * k, QI * S * k + S * WIDE[k])

        def w2_staged(k):
            c = columns(k)
            c0 = c.start if k < W2S else c.start - W2S * 512
            return w2f[:, c0:c0 + c.stop - c.start]

        def half(ap):
            return ap.rearrange("p (g b) -> p g b", b=BG)

        def by_gpsimd(m):
            return m >= F and m % 6 == 0

        def earlier_by_gpsimd(m):
            return sum(by_gpsimd(n) for n in range(m))

        def w1_pair(k):
            return slice(QI * S * k, columns(min(k + 1, NQ - 1)).stop)

        @block.sync
        def _(sp):
            def load_pairs(col, p, n):
                x0 = xt2[0:F, bass.ds(col, GN)]
                lo, hi = XB[n]
                for s in range(SC):
                    if n == 0:
                        sp.dma_start(xa[p][s * F:(s + 1) * F, :], x0).then_inc(s_xp[n], 16)
                    m = min(hi, -(-(SHIFTS - s) // SC)) - lo
                    sp.dma_start(xb[s * F:(s + 1) * F, lo:lo + m, :],
                                 bass.AP(x0.tensor, x0.offset + (s + SC * lo) * N, [[N, F], [SC * N, m], [1, GN]])
                                 ).then_inc(s_xp[n], 16)

            def load_columns(tile, p):
                sp.dma_start(xg[p][:, :, :], xn[:, bass.ds(tile, TG), :]).then_inc(s_x[p], 16)

            load_pairs(0, 0, 0)
            load_pairs(0, 0, 1)
            load_columns(0, 0)
            for n, (lo, hi) in enumerate(XB):
                sp.wait_ge(s_z, hi)
                load_pairs(GN, 1, n)
            load_columns(TG, 1)

            def body(r, first, last):
                for p in range(PG):
                    g = r * PG + p
                    col, tile, before = (v if isinstance(v, int) else sp.snap(v)
                                         for v in ((g + 2) * GN, (g + 1) * TG, g - 1))
                    if not (first and p == 0):
                        if first:
                            sp.wait_ge(s_wl, NQ)
                        sp.wait_ge(s_ge, g * TG)
                        sp.dma_start(G[:, bass.ds(before, 1), :, :], gg[1 - p][:, :, :]).then_inc(s_gs[1 - p], 16)
                        if not (last and p == PG - 1):
                            load_columns(tile, 1 - p)
                    if not last:
                        for n, (lo, hi) in enumerate(XB):
                            sp.wait_ge(s_z, (g + 1) * NCH + hi)
                            load_pairs(col, p, n)
                    elif p == 0:
                        sp.wait_ge(s_z, NG * NCH)
                        sp.dma_start(w2f[:, 0:W2S * 512], w2[:, 0:W2S * 512]).then_inc(s_w2in[0], 16)

            bodies(sp, body)
            sp.wait_ge(s_wl, NQ + NQ - W2S)
            sp.dma_start(w2f[:, 0:F * S - W2S * 512], w2[:, W2S * 512:F * S]).then_inc(s_w2in[1], 16)
            sp.wait_ge(s_ge, NT)
            sp.dma_start(G[:, NG - 1:NG, :, :], gg[(NG - 1) % 2][:, :, :]).then_inc(s_gs[(NG - 1) % 2], 16)
            for bt in range(B // P):
                sp.wait_ge(s_yo, bt + 1)
                sp.dma_start(out[bt * P:(bt + 1) * P, :], osb[:, bt, 0:2 * S]).then_inc(s_out, 16)
            sp.wait_ge(s_out, 16 * (B // P))

        @block.scalar
        def _(act):
            act.dma_start(w0a, w0p).then_inc(s_w0in, 16)
            act.dma_start(w0b, w0q).then_inc(s_w0in, 16)
            act.dma_start(b0c[:, :], b0).then_inc(s_const, 16)
            act.dma_start(b2c[:, :], b2).then_inc(s_const, 16)
            for p in range(2):
                act.dma_start(slots[p][:, BIAS, :], b1.partition_broadcast(P)).then_inc(s_const, 16)
            act.dma_start(msk[:, :], mask).then_inc(s_const, 16)
            act.dma_start(idn[:, :], ident).then_inc(s_const, 16)
            for k in range(0, NQ, 2):
                act.dma_start(w1f[:, w1_pair(k)], w1[:, w1_pair(k)]).then_inc(s_w1in[k // 2], 16)

            def round_pairs(g, c, p):
                e = (p + c) % 2
                act.wait_ge(s_z, g * NCH + (c + 1))
                if not (isinstance(g, int) and g == 0 and c < 2):
                    act.wait_ge(s_l0, g * NCH + (c - 1))
                nc.scalar.activation(zh[e][0:ROWS[c], :], zf[e][0:ROWS[c], :], ACT.Copy).then_inc(s_zh, 1)

            def round_h0(g, p):
                act.wait_ge(s_l0, (g + 1) * NCH)
                nc.scalar.activation(h0h[p][:, :], bankh[:, :], ACT.Identity,
                                     bias=b0c[:, 0:1]).then_inc(s_h0h, 1)

            def copy_g(t, ti):
                q, p = ti % TG, ti // TG % 2
                act.wait_ge(s_g, t + 1)
                nc.scalar.activation(gg[p][:, :, q * BT:(q + 1) * BT],
                                     bankg[:, 0:GC * BT].rearrange("p (c b) -> p c b", b=BT),
                                     ACT.Copy).then_inc(s_ge, 1)

            def round_w1(k):
                act.wait_ge(s_w1in[k // 2], 16)
                nc.scalar.activation(wh[:, columns(k)], w1f[:, columns(k)], ACT.Copy).then_inc(s_wh, 1)

            act.wait_ge(s_mk, 3)
            nc.scalar.activation(b2d[:, :], one[:, :], ACT.Identity).then_inc(s_b2, 1)
            act.wait_ge(s_w0, 1)
            nc.scalar.activation(w0h[:, :, :], w0f, ACT.Copy).then_inc(s_w0, 1)
            for c in range(NCH):
                round_pairs(0, c, 0)
                if c >= NCH - 3:
                    round_w1(c - (NCH - 3))
            act.wait_ge(s_const, 16 * 6)
            round_h0(0, 0)
            for k in range(3, NQ):
                round_w1(k)
            for c in early(ROUND_U):
                round_pairs(1, c, 1)
            act.wait_ge(s_b2, 1)
            nc.scalar.mul(b2d[:, :], b2c[:, :], float(D)).then_inc(s_b2, 1)

            def round_w2(k):
                act.wait_ge(s_t, NG * GQ - NQ + k + 1)
                act.wait_ge(s_w2in[k >= W2S], 16)
                nc.scalar.activation(wh[:, columns(k)], w2_staged(k), ACT.Copy).then_inc(s_wh, 1)

            def body(r, first, last):
                for g, p, q, t, ti in turns(r):
                    if q == 0:
                        act.wait_ge(s_x[p], (r + 1) * 16)
                    for k in range(NQ):
                        u = q * NQ + k
                        if k in SQ:
                            n = SQ.index(k)
                            act.wait_ge(s_t, g * GQ + (u + 1))
                            if n == 0 and not (first and ti == 0):
                                act.wait_ge(s_v, t * VOPS + (QI - VOPS))
                            elif n < NS - 1 and not (first and ti == 0):
                                act.wait_ge(s_q, t * ADDS + (max(n - 1, 1) - ADDS))
                            elif n == NS - 1 and not (first and ti < 2):
                                act.wait_ge(s_f, t * FOLD + (1 - 2 * FOLD))
                            bank = banks[(ti * NS + n) % RING]
                            for m in range(WIDE[k]):
                                i = QI * k + m
                                to = prod[:, n, m * S:(m + 1) * S] if n < NS - 1 else slots[ti % 2][:, RAW + m, :]
                                a = nc.scalar.activation(to, bank[:, m * S:(m + 1) * S], ACT.Copy,
                                                         scale=xg[p][:, q, i:i + 1])
                            a.then_inc(s_s, 1)
                        c, ahead = chunk_steps(ROUND_U).get(u, (0, 0))
                        if ahead and not (last and p + ahead >= PG):
                            round_pairs(g + ahead, c, (p + ahead) % 2)
                        if u == H0_ROUND_AT and not (last and p == PG - 1):
                            round_h0(g + 1, 1 - p)
                        if last and ti == TG * PG - 1 and W2_ROUND_AT.get(k, 1) % 2 == 0:
                            round_w2(W2_ROUND_AT[k])
                        if k == COPY_G_AT and not (first and ti < 2):
                            if q == 2 and not first:
                                act.wait_ge(s_gs[p], r * 16)
                            copy_g(t - 2, (ti - 2) % (TG * PG))

            bodies(act, body)
            for h in range(2):
                act.wait_ge(s_gs[0], 16 * (h + 1) * HG // 2)
                act.wait_ge(s_gs[1], 16 * (h + 1) * HG // 2)
                for i in range(F):
                    m = h * F + i
                    if h == 0 and i % (2 * QI) == QI and i // QI + 3 < NQ:
                        round_w2(i // QI + 3)
                    if m >= GR:
                        act.wait_ge(s_gu, m - GR + 1)
                    nc.scalar.activation(half(gh[m % GR]), G[:, h * HG:(h + 1) * HG, i, :],
                                         ACT.Copy).then_inc(s_gh, 1)
                    if h == 0 and i in LATE_COPY:
                        t = NT - 2 + LATE_COPY.index(i)
                        copy_g(t, t % (TG * PG))
                    if h == 1 and i == 4:
                        act.wait_ge(s_b2, 2)
                        act.wait_ge(s_gu, F)
                        act.wait_ge(s_f, NT * FOLD)
                        nc.scalar.activation(half(y1s), G[:, :, F, :], ACT.Copy).then_inc(s_yc, 1)
                        nc.scalar.activation(y2s[:, 0:HB], bankv[0][:, 0:HB], ACT.Identity,
                                             bias=b2d[:, 0:1]).then_inc(s_yc, 1)
            act.wait_ge(s_gu, 2 * F)
            nc.scalar.activation(y2s[:, HB:B], bankv[1][:, 0:HB], ACT.Identity,
                                 bias=b2d[:, 0:1]).then_inc(s_yc, 1)

        @block.vector
        def _(dve):
            def pairs(g, c, p):
                e = (p + c) % 2
                for n, (lo, hi) in enumerate(XB):
                    if c == lo:
                        dve.wait_ge(s_xp[n], (g + 1) * 16 * SC * (2 - n))
                if not (isinstance(g, int) and g == 0 and c < 2):
                    dve.wait_ge(s_zl, g * NCH + (c - 1))
                nc.vector.tensor_tensor(zf[e][0:ROWS[c], :], xa[p][0:ROWS[c], :], xb[0:ROWS[c], c, :],
                                        ALU.mult).then_inc(s_z, 1)

            def split_first(c):
                dve.wait_ge(s_zh, c + 1)
                nc.vector.tensor_tensor(zl[c % 2][0:ROWS[c], :], zf[c % 2][0:ROWS[c], :],
                                        zh[c % 2][0:ROWS[c], :].bitcast(f32), ALU.subtract).then_inc(s_zl, 1)

            def split_h0(g, p):
                dve.wait_ge(s_h0h, g + 1)
                nc.vector.scalar_tensor_tensor(out=h0l[p][:, :], in0=bankh[:, :], scalar=b0c[:, 0:1],
                                               in1=h0h[p][:, :].bitcast(f32), op0=ALU.add,
                                               op1=ALU.subtract).then_inc(s_h0l, 1)

            def fold(t, a, step):
                if step == 0:
                    dve.wait_ge(s_s, (t + 1) * NS)
                    dve.wait_ge(s_q, (t + 1) * ADDS)
                    dve.wait_ge(s_v, (t + 1) * VOPS)
                    if not (isinstance(t, int) and t == 0):
                        dve.wait_ge(s_f, t * FOLD)
                    nc.vector.tensor_reduce(h1[:, :], slots[a][:, :, :].rearrange("p c s -> p s c"),
                                            AX.X, ALU.add).then_inc(s_f, 1)
                elif step == 1:
                    dve.wait_ge(s_f, t * FOLD + 1)
                    if not (isinstance(t, int) and t == 0):
                        dve.wait_ge(s_g, t)
                    nc.vector.tensor_copy(h1h[:, :], h1[:, :]).then_inc(s_f, 1)
                else:
                    dve.wait_ge(s_f, t * FOLD + 2)
                    nc.vector.tensor_tensor(h1l[:, :], h1[:, :], h1h[:, :].bitcast(f32),
                                            ALU.subtract).then_inc(s_f, 1)

            dve.wait_ge(s_w0in, 32)
            nc.vector.tensor_tensor(w0f, w0a, w0b, ALU.add).then_inc(s_w0, 1)
            for c in range(NCH):
                pairs(0, c, 0)
                if c >= 1:
                    split_first(c - 1)
            split_first(NCH - 1)
            for k in range(NQ):
                dve.wait_ge(s_wh, k + 1)
                nc.vector.tensor_tensor(wl[:, columns(k)], w1f[:, columns(k)], wh[:, columns(k)].bitcast(f32),
                                        ALU.subtract).then_inc(s_wl, 1)
                if k == 0:
                    dve.wait_ge(s_const, 16 * 6)
                    split_h0(0, 0)
            for c in early(PAIRS_U):
                pairs(1, c, 1)

            def round_w2(k):
                dve.wait_ge(s_t, NG * GQ - NQ + k + 1)
                dve.wait_ge(s_w2in[k >= W2S], 16)
                nc.vector.tensor_copy(wh[:, columns(k)], w2_staged(k)).then_inc(s_wv, 1)

            def body(r, first, last):
                for g, p, q, t, ti in turns(r):
                    a = ti % 2
                    if q == 0:
                        dve.wait_ge(s_x[p], (r + 1) * 16)
                    for k in range(NQ):
                        u = q * NQ + k
                        if k in VQ:
                            n = VQ.index(k)
                            dve.wait_ge(s_t, g * GQ + (u + 1))
                            if n == 0:
                                dve.wait_ge(s_s, t * NS + 1)
                            for m in range(QI):
                                i = QI * k + m
                                if n:
                                    dve.wait_ge(s_v, t * VOPS + (QI * (n - 1) + m + 1))
                                part = slots[a][:, ACC + m, :]
                                nc.vector.scalar_tensor_tensor(
                                    out=part, in0=bankv[(ti * NV + n) % RING][:, m * S:(m + 1) * S],
                                    scalar=xg[p][:, q, i:i + 1],
                                    in1=part if n else prod[:, 0, m * S:(m + 1) * S],
                                    op0=ALU.mult, op1=ALU.add).then_inc(s_v, 1)
                        c, ahead = chunk_steps(PAIRS_U).get(u, (0, 0))
                        if ahead and not (last and p + ahead >= PG):
                            pairs(g + ahead, c, (p + ahead) % 2)
                        if u == H0_SPLIT_AT and not (last and p == PG - 1):
                            split_h0(g + 1, 1 - p)
                        if last and ti == TG * PG - 1 and W2_ROUND_AT.get(k, 0) % 2:
                            round_w2(W2_ROUND_AT[k])
                        if k in FOLD_AT and not (first and ti == 0):
                            fold(t - 1, 1 - a, FOLD_AT.index(k))

            bodies(dve, body)
            for h in range(2):
                for i in range(F):
                    m = h * F + i
                    if h == 0 and i % (2 * QI) == 0 and i // QI + 3 < NQ:
                        round_w2(i // QI + 3)
                    if not by_gpsimd(m):
                        dve.wait_ge(s_gh, m + 1)
                        nc.vector.tensor_tensor(half(gl[m % GR]), G[:, h * HG:(h + 1) * HG, i, :],
                                                half(gh[m % GR]).bitcast(f32), ALU.subtract).then_inc(s_gl, 1)
                    if h == 0 and i in LATE_FOLD:
                        fold(NT - 1, (NT - 1) % 2, LATE_FOLD.index(i))
            for bt in range(B // P):
                dve.wait_ge(s_yt, bt + 1)
                nc.vector.tensor_copy(osb[:, bt, 0:2 * S], banks[bt % 2][:, 0:2 * S]).then_inc(s_yo, 1)

        @block.gpsimd
        def _(pool):
            for p in range(2):
                nc.gpsimd.memset(xblk[p][:, :, :, :].bitcast(f32), 0.0).then_inc(s_mk, 1)
            nc.gpsimd.memset(one[:, :], 1.0).then_inc(s_mk, 1)
            pool.wait_ge(s_w0, 2)
            nc.gpsimd.tensor_tensor(w0l[:, :, :], w0f, w0h[:, :, :].bitcast(f32), ALU.subtract).then_inc(s_w0, 1)
            pool.wait_ge(s_mk, 3)
            pool.wait_ge(s_const, 16 * 6)
            for p in range(2):
                nc.gpsimd.tensor_copy(xblk[p][:, 0, F, :], msk[:, :]).then_inc(s_mk, 1)

            def split_pairs(g, c, p):
                e = (p + c) % 2
                pool.wait_ge(s_zh, g * NCH + (c + 1))
                nc.gpsimd.tensor_tensor(zl[e][0:ROWS[c], :], zf[e][0:ROWS[c], :],
                                        zh[e][0:ROWS[c], :].bitcast(f32), ALU.subtract).then_inc(s_zl, 1)

            for c in early(SPLIT_U):
                split_pairs(1, c, 1)

            def split_w2(k):
                if k % 2:
                    pool.wait_ge(s_wv, k // 2 + 1)
                else:
                    pool.wait_ge(s_wh, NQ + k // 2 + 1)
                nc.gpsimd.tensor_tensor(wl[:, columns(k)], w2_staged(k), wh[:, columns(k)].bitcast(f32),
                                        ALU.subtract).then_inc(s_wl, 1)

            def body(r, first, last):
                for g, p, q, t, ti in turns(r):
                    a = ti % 2
                    sums = slots[a][:, SUM:SUM + QI, :].rearrange("p c s -> p (c s)")
                    if q == 0:
                        pool.wait_ge(s_x[p], (r + 1) * 16)
                        nc.gpsimd.tensor_tensor(xs[p][:, :, 0, :].bitcast(f32r), xg[p][:, :, :],
                                                one[:, :].unsqueeze(2).broadcast_to([P, TG, F]),
                                                ALU.mult).then_inc(s_xs, 1)
                        pool.wait_ge(s_xs, 2 * g + 1)
                        nc.gpsimd.tensor_tensor(xs[p][:, :, 1, :], xg[p][:, :, :], xs[p][:, :, 0, :],
                                                ALU.subtract).then_inc(s_xs, 1)
                        pool.wait_ge(s_xs, 2 * g + 2)
                    for k in range(NQ):
                        u = q * NQ + k
                        if k in SUM_AT:
                            n = SUM_AT.index(k) + 2
                            pool.wait_ge(s_s, t * NS + (n + 1))
                            if n == 2:
                                if not (first and ti < 2):
                                    pool.wait_ge(s_f, t * FOLD + (1 - 2 * FOLD))
                                nc.gpsimd.tensor_tensor(sums, prod[:, 1, :], prod[:, 2, :],
                                                        ALU.add).then_inc(s_q, 1)
                            else:
                                pool.wait_ge(s_q, t * ADDS + (n - 2))
                                nc.gpsimd.tensor_tensor(sums, sums, prod[:, n, :], ALU.add).then_inc(s_q, 1)
                        c, ahead = chunk_steps(SPLIT_U).get(u, (0, 0))
                        if ahead and not (last and p + ahead >= PG):
                            split_pairs(g + ahead, c, (p + ahead) % 2)
                        if last and ti == TG * PG - 1 and k in W2_SPLIT_AT:
                            split_w2(W2_SPLIT_AT[k])
                        if k == BLOCKS_AT:
                            if first and ti < 2:
                                pool.wait_ge(s_mk, 5)
                            else:
                                pool.wait_ge(s_g, t - 1)
                            nc.gpsimd.tensor_tensor(
                                xblk[a][:, :, 0:F, :], xs[p][:, q, :, :].unsqueeze(3).broadcast_to([P, 2, F, BT]),
                                msk[:, :].unsqueeze(1).unsqueeze(1).broadcast_to([P, 2, F, BT]),
                                ALU.mult).then_inc(s_xk, 1)

            bodies(pool, body)
            for k in range(NQ):
                if k not in W2_SPLIT_AT.values():
                    split_w2(k)
            for m in range(F, 2 * F):
                if by_gpsimd(m):
                    pool.wait_ge(s_gh, m + 1)
                    nc.gpsimd.tensor_tensor(half(gl[m % GR]), G[:, HG:NG, m - F, :],
                                            half(gh[m % GR]).bitcast(f32), ALU.subtract).then_inc(s_gp, 1)

        @block.tensor
        def _(pe):
            def product(o, ah, al, bh, bl, start=True, stop=True):
                nc.tensor.matmul(o, ah, bh, start=start, stop=False)
                nc.tensor.matmul(o, ah, bl, start=False, stop=False)
                return nc.tensor.matmul(o, al, bh, start=False, stop=stop)

            def layer0(g, c, p):
                n, e = ROWS[c], (p + c) % 2
                pe.wait_ge(s_zl, g * NCH + (c + 1))
                product(bankh[:, :], w0h[0:n, c, :], w0l[0:n, c, :], zh[e][0:n, :], zl[e][0:n, :],
                        start=(c == 0), stop=(c == NCH - 1)).then_inc(s_l0, 1)

            def into_g(t, a):
                pe.wait_ge(s_f, (t + 1) * FOLD)
                pe.wait_ge(s_xk, t + 1)
                if not (isinstance(t, int) and t == 0):
                    pe.wait_ge(s_ge, t)
                product(bankg[:, 0:GC * BT], h1h[:, :], h1l[:, :],
                        xblk[a][:, 0, :, :].rearrange("p c b -> p (c b)"),
                        xblk[a][:, 1, :, :].rearrange("p c b -> p (c b)")).then_inc(s_g, 1)

            pe.wait_ge(s_w0, 3)
            for c in range(NCH):
                layer0(0, c, 0)

            def body(r, first, last):
                for g, p, q, t, ti in turns(r):
                    for k in range(NQ):
                        u = q * NQ + k
                        if u == 0:
                            pe.wait_ge(s_h0l, g + 1)
                        if first and ti == 0:
                            pe.wait_ge(s_wl, k + 1)
                        if k in VQ:
                            index = ti * NV + VQ.index(k)
                            before = last_use(index, RING, VBODY)
                            if not (first and before < 0):
                                pe.wait_ge(s_v, t * VOPS + QI * (before + 1 - ti * NV))
                            bank = bankv[index % RING]
                        else:
                            index = ti * NS + SQ.index(k)
                            before = last_use(index, RING, SBODY)
                            if not (first and before < 0):
                                pe.wait_ge(s_s, t * NS + (before + 1 - ti * NS))
                            bank = banks[index % RING]
                        columns_q = slice(q * P, (q + 1) * P)
                        product(bank[:, 0:S * WIDE[k]], h0h[p][:, columns_q], h0l[p][:, columns_q],
                                wh[:, columns(k)], wl[:, columns(k)]).then_inc(s_t, 1)
                        c, ahead = chunk_steps(LAYER0_U).get(u, (0, 0))
                        if ahead and not (last and p + ahead >= PG):
                            if c == 0:
                                pe.wait_ge(s_h0l, g + 1)
                            layer0(g + ahead, c, (p + ahead) % 2)
                        if k == INTO_G_AT and not (first and ti < 2):
                            into_g(t - 2, ti % 2)

            bodies(pe, body)
            for h in range(2):
                for i in range(F):
                    m = h * F + i
                    if h == 0 and i % QI == 0:
                        pe.wait_ge(s_wl, NQ + i // QI + 1)
                    if by_gpsimd(m):
                        pe.wait_ge(s_gp, earlier_by_gpsimd(m) + 1)
                    else:
                        pe.wait_ge(s_gl, m - earlier_by_gpsimd(m) + 1)
                    product(bankv[h][:, 0:HB], wh[:, i * S:(i + 1) * S], wl[:, i * S:(i + 1) * S],
                            gh[m % GR], gl[m % GR], start=(i == 0), stop=(i == F - 1)).then_inc(s_gu, 1)
                    if h == 0 and i in LATE:
                        t = NT - 2 + LATE.index(i)
                        into_g(t, t % 2)
            for bt in range(B // P):
                if bt == 0:
                    pe.wait_ge(s_yc, 2)
                if bt * P == HB:
                    pe.wait_ge(s_yc, 3)
                if bt >= 2:
                    pe.wait_ge(s_yo, bt - 1)
                nc.tensor.transpose(banks[bt % 2][:, 0:S], y1s[:, bt * P:(bt + 1) * P], idn[:, :])
                nc.tensor.transpose(banks[bt % 2][:, S:2 * S], y2s[:, bt * P:(bt + 1) * P],
                                    idn[:, :]).then_inc(s_yt, 1)


def kernel(r_x, L0_rec_w0, L0_rec_b0, L0_rec_w1, L0_rec_b1, L0_rec_w2, L0_rec_b2):
    import numpy as np
    import concourse.bacc as bacc
    from concourse.bass_utils import run_bass_kernel_spmd

    x = np.asarray(r_x)
    xt = x.transpose(1, 0, 2).reshape(F, N)
    w0 = np.asarray(L0_rec_w0).reshape(F, F, S)
    w0p = np.zeros((R, NCH, S), w0.dtype)
    w0q = np.zeros((R, NCH, S), w0.dtype)
    i = np.arange(F)
    for k in range(SHIFTS):
        c, r = divmod(k, SC)
        w0p[r * F:(r + 1) * F, c] = w0[i, (i + k) % F]
        if k:
            w0q[r * F:(r + 1) * F, c] = w0[(i + k) % F, i]
    arrays = {
        "xt2": np.concatenate([xt, xt[:SC * NCH]], axis=0),
        "xn": x.reshape(NT, BT, F, D).transpose(1, 3, 0, 2).reshape(P, NT, F),
        "w0p": w0p,
        "w0q": w0q,
        "w1": np.asarray(L0_rec_w1).reshape(F, S, S).transpose(1, 0, 2).reshape(S, F * S),
        "w2": np.asarray(L0_rec_w2).reshape(F, S, S).transpose(1, 0, 2).reshape(S, F * S),
        "b0": np.asarray(L0_rec_b0).reshape(S, 1),
        "b1": np.asarray(L0_rec_b1).reshape(S),
        "b2": np.asarray(L0_rec_b2).reshape(S, 1),
        "mask": np.kron(np.eye(BT, dtype=np.float32), np.ones((D, 1), np.float32)),
        "ident": np.eye(P, dtype=np.float32),
    }
    nc = bacc.Bacc("TRN2", target_bir_lowering=False, num_devices=1)
    ins, args = {}, []
    for name, a in arrays.items():
        ins[f"in_{name}"] = np.ascontiguousarray(a)
        args.append(nc.dram_tensor(f"in_{name}", a.shape, mybir.dt.from_np(a.dtype), kind="ExternalInput").ap())
    args.append(nc.dram_tensor("out_y", (B, 2 * S), mybir.dt.float32, kind="ExternalOutput").ap())
    build(nc, *args)
    r = run_bass_kernel_spmd(nc, [ins], core_ids=[0])
    return r.results[0]["out_y"]
```

```python
import concourse.bass as bass
from concourse import mybir
from contextlib import ExitStack


B, F, D, S = 512, 39, 16, 128
P = 128
N = B * D
NT = N // P
TG = 4
NG = NT // TG
GN = TG * P
BT = P // D
BG = TG * BT
PG = 2

SHIFTS = F // 2 + 1
SC = P // F
R = F * SC
MCH = SHIFTS // SC
X0 = SC * MCH
KX = F + 1 - 2 * X0
TOP = P - R
REST = F - X0 - TOP
LR = KX * REST
NCH = MCH + 1
ROWS = [P if c < KX else R for c in range(MCH)] + [3 * LR]
XB = [(0, 2), (2, MCH), (MCH, NCH)]

QI = 4
NQ = -(-F // QI)
WIDE = [min(QI, F - QI * k) for k in range(NQ)]
GQ = TG * NQ
VQ = [1, 4, 6, 8]
SQ = [0, 2, 3, 5, 7, 9]
NV, NS = len(VQ), len(SQ)
VOPS = QI * NV
ACC, SUM, RAW = 0, QI, 2 * QI
BIAS = RAW + WIDE[SQ[-1]]
SLOTS = BIAS + 1
ADDS = NS - 3
FOLD = 3
GC = F + 1
RING = 3
VBODY, SBODY = NV * TG * PG, NS * TG * PG

PAIRS_U, ROUND_U, SPLIT_U, LAYER0_U, SPACE = -3, 0, 1, 9, 4


def chunk_steps(u0):
    return {(u0 + SPACE * c) % GQ: (c, 1 if u0 + SPACE * c >= 0 else 2) for c in range(NCH)}


def early(u0):
    return [c for c in range(NCH) if u0 + SPACE * c < 0]


W0C = [slice(0, 2), slice(2, NCH)]
FIRST = [slice(0, P), slice(P, GN)]
W1_AFTER = [4, 4, 5, 6, 6, 6]
W1_GPSIMD = [0, 1, 4, 7]
H0_FIRST_AT = [3, 5]

H0_ROUND_AT, H0_SPLIT_AT = 34, 35
FOLD_AT = [2, 5, 7]
INTO_G_AT = 2
COPY_G_AT = 5
BLOCKS_AT = 0
SUM_AT = [4, 6, 8]

HB = B // 2
HG = NG // 2
W2P = [0, QI, NCH] + list(range(NCH + QI, F, QI)) + [F]
W2N = len(W2P) - 1
W2E = 2
W2S = max(k for k in range(W2N) if S * W2P[k] <= NCH * GN)
W2F = min(k for k in range(W2N) if W2P[k] >= F - W2P[W2S])
GR = 8
G_GPSIMD = 4
G_GPSIMD_FROM = 30
LATE = [5, 15]
LATE_COPY = [7, 23]
Y1_AT = 13
LATE_FOLD = [6, 7, 9]
W2_ROUND_U = {9: 1, 11: 0, 37: 3, 38: 2}
W2_SPLIT_U = {12: 0, 13: 1}
G_ROUND_U = {0: 0, 1: 1, 4: 2, 5: 3, 13: 4, 16: 5}
G_SPLIT_U = {5: 0, 8: 1, 9: 2, 10: 3, 19: 4, 20: 5}
W2_ROUND_I = {4: 4, 8: 5, 16: 6, 20: 7, 23: 9, 24: 8}


def last_use(index, ring, body):
    bank = index % ring
    same = [j for j in range(index) if j % ring == bank]
    return same[-1] if same else max(j for j in range(body) if j % ring == bank) - body


def build(nc, xt2, xn, w0p, w0q, w1, w2, b0, b1, b2, mask, rows, ident, out):
    f32 = mybir.dt.float32
    f32r = mybir.dt.float32r
    ALU = mybir.AluOpType
    ACT = mybir.ActivationFunctionType
    AX = mybir.AxisListType

    ctx = ExitStack()
    with ctx:
        def sb(name, shape, dt=f32):
            return ctx.enter_context(nc.sbuf_tensor(name, shape, dt))

        def pb(name):
            return ctx.enter_context(nc.psum_tensor(name, [P, 512], f32))

        def sem(name):
            return ctx.enter_context(nc.semaphore(name))

        w0h = sb("w0h", [P, NCH, S], f32r)
        w0l = sb("w0l", [P, NCH, S], f32r)
        wh = sb("wh", [P, F * S], f32r)
        wl = sb("wl", [P, F * S], f32r)
        xa = sb("xa", [P, GN])
        xc = sb("xc", [3 * LR, GN])
        xb = sb("xb", [P, NCH, GN])
        xg = [sb(f"xg{p}", [P, TG, F]) for p in range(2)]
        xs = [sb(f"xs{p}", [P, TG, 2, F]) for p in range(2)]
        zf = [sb(f"zf{p}", [P, GN]) for p in range(2)]
        zh = [sb(f"zh{p}", [P, GN], f32r) for p in range(2)]
        zl = [sb(f"zl{p}", [P, GN], f32r) for p in range(2)]
        h0h = [sb(f"h0h{p}", [P, GN], f32r) for p in range(2)]
        h0l = [sb(f"h0l{p}", [P, GN], f32r) for p in range(2)]
        z0h, z0l = [*zh, h0h[1]], [*zl, h0l[1]]
        prod = sb("prod", [P, NS - 1, QI * S])
        slots = [sb(f"slots{p}", [P, SLOTS, S]) for p in range(2)]
        h1 = sb("h1", [P, S])
        h1h = sb("h1h", [P, S], f32r)
        h1l = sb("h1l", [P, S], f32r)
        xblk = [sb(f"xblk{p}", [P, 2, GC, BT], f32r) for p in range(2)]
        gg = [sb(f"gg{p}", [P, GC, BG]) for p in range(2)]
        G = sb("G", [P, NG, GC, BG])
        b0c = sb("b0c", [P, 1])
        b2c = sb("b2c", [P, 1])
        b2d = sb("b2d", [P, 1])
        msk = sb("msk", [P, BT])
        lo_rows = sb("lo_rows", [P, 1])
        idn = sb("idn", [P, P])
        one = sb("one", [P, 1])

        def staged(rows, g, n):
            return G[0:rows, g:g - (-n // (GC * BG)), :, :].rearrange("p g c b -> p (g c b)")[:, 0:n]

        w0a, w0b, w0f = (staged(P, g, NCH * S).rearrange("p (c s) -> p c s", c=NCH) for g in range(3))
        w1f = staged(P, NG + (-F * S // (GC * BG)), F * S)
        w2f = xb[:, :, :].rearrange("p c n -> p (c n)")
        y1s, y2s = (s[:, :, :].rearrange("p c s -> p (c s)")[:, 0:B] for s in slots)
        osb = prod
        gh = [b[:, n * HB:(n + 1) * HB] for b in (h0h[0], *zh, h0h[1]) for n in range(2)]
        gl = [b[:, n * HB:(n + 1) * HB] for b in (h0l[0], *zl, h0l[1]) for n in range(2)]

        bankv = [pb(f"bankv{n}") for n in range(RING)]
        banks = [pb(f"banks{n}") for n in range(RING)]
        banky = [bankv[(VBODY + h) % RING] for h in range(2)]
        bankh = pb("bankh")
        bankg = pb("bankg")

        s_const = sem("const_loaded")
        s_first = sem("b0_and_masks_loaded")
        s_w0in = [sem(f"w0_loaded{n}") for n in range(len(W0C))]
        s_w1in = [sem(f"w1_loaded{k}") for k in range(0, NQ, 2)]
        s_w2in = [sem(f"w2_loaded{n}") for n in range(2)]
        s_x = [sem(f"x_loaded{p}") for p in range(2)]
        s_xp = [sem(f"x_pairs_loaded{n}") for n in range(len(XB))]
        s_xr = [sem(f"x_rest_loaded{n}") for n in range(len(XB))]
        s_w0 = sem("w0_summed")
        s_w0h = sem("w0_rounded")
        s_w0l = sem("w0_split")
        s_wd = sem("w1_split_by_vector")
        s_wh = sem("w_rounded")
        s_wl = sem("w_split")
        s_wv = sem("w2_rounded_by_vector")
        s_b2 = sem("b2_scaled")
        s_z = sem("pairs_made")
        s_zh = sem("pairs_rounded")
        s_zl = sem("pairs_split")
        s_l0 = sem("pairs_used")
        s_h0h = sem("h0_rounded")
        s_h0l = sem("h0_split")
        s_t = sem("quad_ready")
        s_v = sem("products_added")
        s_s = sem("quad_multiplied")
        s_q = sem("products_summed")
        s_f = sem("tile_folded")
        s_xs = sem("x_split")
        s_xk = sem("blocks_ready")
        s_mk = sem("constants_ready")
        s_g = sem("g_ready")
        s_ge = sem("g_copied")
        s_gs = [sem(f"g_stored{p}") for p in range(2)]
        s_gh = sem("g_rounded")
        s_gl = sem("g_split")
        s_gp = sem("g_split_by_gpsimd")
        s_gu = sem("g_used")
        s_yc = sem("y_halves_copied")
        s_yt = sem("y_turned")
        s_yo = sem("y_copied")
        s_out = sem("y_stored")

        block = ctx.enter_context(nc.Block())

        def split_rows(c, hi, lo):
            return (ROWS[c], lo) if c < MCH else (LR, hi)

        def bodies(eng, body):
            body(0, True, False)
            with eng.Fori(1, NG // PG - 1) as r:
                body(r, False, False)
            body(NG // PG - 1, False, True)

        def turns(r):
            for p in range(PG):
                for q in range(TG):
                    g = r * PG + p
                    yield g, p, q, g * TG + q, p * TG + q

        def columns(k):
            return slice(QI * S * k, QI * S * k + S * WIDE[k])

        def w2_staged(k):
            lo, hi = (S * (i - (k >= W2S) * W2P[W2S]) for i in W2P[k:k + 2])
            return w2f[:, lo:hi]

        def w2_split(k):
            c = slice(S * W2P[k], S * W2P[k + 1])
            if k < W2E:
                return tuple(w[:, :, :].rearrange("p c s -> p (c s)")[:, c] for w in (w0h, w0l))
            return wh[:, c], wl[:, c]

        def last_quad(k):
            return (NT - 1) * NQ + (W2P[k + 1] - 1) // QI + 1

        def half(ap):
            return ap.rearrange("p (g b) -> p g b", b=BG)

        def by_gpsimd(m):
            return m >= G_GPSIMD_FROM and m % G_GPSIMD == 0

        def earlier_by_gpsimd(m):
            return sum(by_gpsimd(n) for n in range(m))

        def w1_pair(k):
            return slice(QI * S * k, columns(min(k + 1, NQ - 1)).stop)

        def load_main(eng, col, n):
            x0 = xt2[0:F, bass.ds(col, GN)]
            lo, hi = XB[n]
            if n == 0:
                eng.dma_start(xa[0:R, :], bass.AP(x0.tensor, x0.offset, [[0, SC], [N, F], [1, GN]])
                              ).then_inc(s_xp[n], 16)
            if lo < MCH:
                for s in range(SC):
                    eng.dma_start(xb[s * F:(s + 1) * F, lo:hi, :],
                                  bass.AP(x0.tensor, x0.offset + (s + SC * lo) * N,
                                          [[N, F], [SC * N, hi - lo], [1, GN]])).then_inc(s_xp[n], 16)
            else:
                eng.dma_start(xc[:, :], bass.AP(x0.tensor, x0.offset + TOP * N, [[0, 3 * KX], [N, REST], [1, GN]])
                              ).then_inc(s_xp[n], 16)
                for copy in range(3):
                    eng.dma_start(xb[copy * LR:(copy + 1) * LR, MCH, :],
                                  bass.AP(x0.tensor, x0.offset + (TOP + X0) * N, [[N, KX], [N, REST], [1, GN]])
                                  ).then_inc(s_xp[n], 16)

        def last_reader(n):
            return XB[n][1] if n else MCH

        def loads(n):
            lo = XB[n][0]
            return (SC if lo < MCH else 1 + 3) + (n == 0), (lo < KX) + (n == 0)

        def load_rest(eng, col, n, done):
            x0 = xt2[0:TOP, bass.ds(col, GN)]
            lo, hi = XB[n]
            if n == 0:
                eng.dma_start(xa[R:P, :], x0).then_inc(done, 16)
            if lo < KX:
                m = min(hi, KX) - lo
                eng.dma_start(xb[R:P, lo:lo + m, :],
                              bass.AP(x0.tensor, x0.offset + (X0 + lo) * N, [[N, TOP], [N, m], [1, GN]])
                              ).then_inc(done, 16)

        @block.sync
        def _(sp):
            def load_columns(tile, p):
                sp.dma_start(xg[p][:, :, :], xn[:, bass.ds(tile, TG), :]).then_inc(s_x[p], 16)

            for n in range(len(XB)):
                load_main(sp, 0, n)
            for k in range(0, NQ, 2):
                sp.dma_start(w1f[:, w1_pair(k)], w1[:, w1_pair(k)]).then_inc(s_w1in[k // 2], 16)
            load_columns(0, 0)
            sp.dma_start(b2c[:, :], b2).then_inc(s_const, 16)
            for p in range(2):
                sp.dma_start(slots[p][:, BIAS, :], b1.partition_broadcast(P)).then_inc(s_const, 16)
            sp.dma_start(idn[:, :], ident).then_inc(s_const, 16)
            for n, (lo, hi) in enumerate(XB):
                sp.wait_ge(s_z, last_reader(n))
                load_main(sp, GN, n)
                load_rest(sp, GN, n, s_xp[n])
            load_columns(TG, 1)

            def body(r, first, last):
                for p in range(PG):
                    g = r * PG + p
                    col, tile, before = (v if isinstance(v, int) else sp.snap(v)
                                         for v in ((g + 2) * GN, (g + 1) * TG, g - 1))
                    if not (first and p == 0):
                        if first:
                            sp.wait_ge(s_wl, len(W1_GPSIMD))
                            sp.wait_ge(s_wd, NQ - len(W1_GPSIMD))
                        sp.wait_ge(s_ge, g * TG)
                        sp.dma_start(G[:, bass.ds(before, 1), :, :], gg[1 - p][:, :, :]).then_inc(s_gs[1 - p], 16)
                        if not (last and p == PG - 1):
                            load_columns(tile, 1 - p)
                    if not last:
                        for n, (lo, hi) in enumerate(XB):
                            sp.wait_ge(s_z, (g + 1) * NCH + last_reader(n))
                            load_main(sp, col, n)
                            load_rest(sp, col, n, s_xp[n])
                    elif p == 0:
                        sp.wait_ge(s_z, NG * NCH)
                        sp.dma_start(w2f[:, 0:S * W2P[W2S]], w2[:, 0:S * W2P[W2S]]).then_inc(s_w2in[0], 16)

            bodies(sp, body)
            sp.wait_ge(s_wl, len(W1_GPSIMD) + W2F)
            sp.dma_start(w2f[:, 0:S * (F - W2P[W2S])], w2[:, S * W2P[W2S]:S * F]).then_inc(s_w2in[1], 16)
            sp.wait_ge(s_ge, NT)
            sp.dma_start(G[:, NG - 1:NG, :, :], gg[(NG - 1) % 2][:, :, :]).then_inc(s_gs[(NG - 1) % 2], 16)
            for bt in range(B // P):
                sp.wait_ge(s_yo, bt + 1)
                sp.dma_start(out[bt * P:(bt + 1) * P, :], osb[:, bt, 0:2 * S]).then_inc(s_out, 16)
            sp.wait_ge(s_out, 16 * (B // P))

        @block.scalar
        def _(act):
            def load_w0(n):
                act.dma_start(w0a[:, W0C[n], :], w0p[:, W0C[n], :]).then_inc(s_w0in[n], 16)
                act.dma_start(w0b[:, W0C[n], :], w0q[:, W0C[n], :]).then_inc(s_w0in[n], 16)

            load_w0(0)
            act.wait_ge(s_mk, 1)
            nc.scalar.activation(b2d[:, :], one[:, :], ACT.Identity).then_inc(s_b2, 1)
            load_w0(1)

            def round_pairs(g, c, p):
                e = (p + c) % 2
                act.wait_ge(s_z, g * NCH + (c + 1))
                act.wait_ge(s_l0, g * NCH + (c - 1))
                nc.scalar.activation(zh[e][0:ROWS[c], :], zf[e][0:ROWS[c], :], ACT.Copy).then_inc(s_zh, 1)

            def round_h0(g, p, n=slice(0, GN)):
                act.wait_ge(s_l0, (g + 1) * NCH)
                nc.scalar.activation(h0h[p][:, n], bankh[:, n], ACT.Identity,
                                     bias=b0c[:, 0:1]).then_inc(s_h0h, 1)

            def copy_g(t, ti):
                q, p = ti % TG, ti // TG % 2
                act.wait_ge(s_g, t + 1)
                nc.scalar.activation(gg[p][:, :, q * BT:(q + 1) * BT],
                                     bankg[:, 0:GC * BT].rearrange("p (c b) -> p c b", b=BT),
                                     ACT.Copy).then_inc(s_ge, 1)

            def round_w1(k):
                act.wait_ge(s_w1in[k // 2], 16)
                nc.scalar.activation(wh[:, columns(k)], w1f[:, columns(k)], ACT.Copy).then_inc(s_wh, 1)

            def round_w0(n):
                c = slice(W0C[n].start, min(W0C[n].stop, MCH))
                act.wait_ge(s_w0, n + 1)
                nc.scalar.activation(w0h[:, c, :], w0f[:, c, :], ACT.Copy).then_inc(s_w0h, 1)

            round_w0(0)
            for c in range(NCH):
                if c == 2:
                    round_w0(1)
                act.wait_ge(s_z, c + 1)
                if c >= 3:
                    act.wait_ge(s_l0, c - 2)
                nc.scalar.activation(z0h[c % 3][0:ROWS[c], :], zf[c % 2][0:ROWS[c], :], ACT.Copy).then_inc(s_zh, 1)
                for k, after in enumerate(W1_AFTER):
                    if after == c:
                        round_w1(k)
            act.wait_ge(s_first, 48)
            for n in FIRST:
                if n.start:
                    act.wait_ge(s_h0l, 1)
                round_h0(0, 0, n)
            for k in range(len(W1_AFTER), NQ):
                round_w1(k)
            for c in early(ROUND_U):
                round_pairs(1, c, 1)
            act.wait_ge(s_b2, 1)
            act.wait_ge(s_const, 16 * 4)
            nc.scalar.mul(b2d[:, :], b2c[:, :], float(D)).then_inc(s_b2, 1)

            def round_w2(k):
                if k >= W2E:
                    act.wait_ge(s_t, last_quad(k))
                else:
                    act.wait_ge(s_l0, NG * NCH)
                act.wait_ge(s_w2in[k >= W2S], 16)
                nc.scalar.activation(w2_split(k)[0], w2_staged(k), ACT.Copy).then_inc(s_wh, 1)

            def round_g(m):
                h, i = m // F, m % F
                if i == 0:
                    act.wait_ge(s_gs[0], 16 * (h + 1) * HG // 2)
                    act.wait_ge(s_gs[1], 16 * (h + 1) * HG // 2)
                if m >= GR:
                    act.wait_ge(s_gu, m - GR + 1)
                nc.scalar.activation(half(gh[m % GR]), G[:, h * HG:(h + 1) * HG, i, :],
                                     ACT.Copy).then_inc(s_gh, 1)

            def body(r, first, last):
                for g, p, q, t, ti in turns(r):
                    if q == 0:
                        act.wait_ge(s_x[p], (r + 1) * 16)
                    for k in range(NQ):
                        u = q * NQ + k
                        if k in SQ:
                            n = SQ.index(k)
                            act.wait_ge(s_t, g * GQ + (u + 1))
                            if n == 0 and not (first and ti == 0):
                                act.wait_ge(s_v, t * VOPS + (QI - VOPS))
                            elif n < NS - 1 and not (first and ti == 0):
                                act.wait_ge(s_q, t * ADDS + (max(n - 1, 1) - ADDS))
                            elif n == NS - 1 and not (first and ti < 2):
                                act.wait_ge(s_f, t * FOLD + (1 - 2 * FOLD))
                            bank = banks[(ti * NS + n) % RING]
                            for m in range(WIDE[k]):
                                i = QI * k + m
                                to = prod[:, n, m * S:(m + 1) * S] if n < NS - 1 else slots[ti % 2][:, RAW + m, :]
                                a = nc.scalar.activation(to, bank[:, m * S:(m + 1) * S], ACT.Copy,
                                                         scale=xg[p][:, q, i:i + 1])
                            a.then_inc(s_s, 1)
                        c, ahead = chunk_steps(ROUND_U).get(u, (0, 0))
                        if ahead and not (last and p + ahead >= PG):
                            round_pairs(g + ahead, c, (p + ahead) % 2)
                        if u == H0_ROUND_AT and not (last and p == PG - 1):
                            round_h0(g + 1, 1 - p)
                        if last and p == PG - 1 and W2_ROUND_U.get(u, 1) % 2 == 0:
                            round_w2(W2_ROUND_U[u])
                        if last and p == PG - 1 and u in G_ROUND_U:
                            round_g(G_ROUND_U[u])
                        if k == COPY_G_AT and not (first and ti < 2):
                            if q == 2 and not first:
                                act.wait_ge(s_gs[p], r * 16)
                            copy_g(t - 2, (ti - 2) % (TG * PG))

            bodies(act, body)
            for h in range(2):
                for i in range(F):
                    if h == 0 and W2_ROUND_I.get(i, 1) % 2 == 0:
                        round_w2(W2_ROUND_I[i])
                    if h * F + i not in G_ROUND_U.values():
                        round_g(h * F + i)
                    if h == 0 and i in LATE_COPY:
                        t = NT - 2 + LATE_COPY.index(i)
                        copy_g(t, t % (TG * PG))
                    if h == 1 and i == Y1_AT:
                        act.wait_ge(s_b2, 2)
                        act.wait_ge(s_gu, F)
                        act.wait_ge(s_f, NT * FOLD)
                        nc.scalar.activation(half(y1s), G[:, :, F, :], ACT.Copy).then_inc(s_yc, 1)
                        nc.scalar.activation(y2s[:, 0:HB], banky[0][:, 0:HB], ACT.Identity,
                                             bias=b2d[:, 0:1]).then_inc(s_yc, 1)
            act.wait_ge(s_gu, 2 * F)
            nc.scalar.activation(y2s[:, HB:B], banky[1][:, 0:HB], ACT.Identity,
                                 bias=b2d[:, 0:1]).then_inc(s_yc, 1)

        @block.vector
        def _(dve):
            def pairs(g, c, p):
                e = (p + c) % 2
                for n, (lo, hi) in enumerate(XB):
                    if c == lo:
                        main, rest = loads(n)
                        dve.wait_ge(s_xp[n], g * 16 * (main + rest) + 16 * main)
                        if isinstance(g, int) and g == 0 and rest:
                            dve.wait_ge(s_xr[n], 16 * rest)
                if not (isinstance(g, int) and g == 0 and c < 2):
                    dve.wait_ge(s_zl, g * NCH + (c - 1))
                nc.vector.tensor_tensor(zf[e][0:ROWS[c], :], (xa if c < MCH else xc)[0:ROWS[c], :],
                                        xb[0:ROWS[c], c, :], ALU.mult).then_inc(s_z, 1)

            def split_first(c):
                dve.wait_ge(s_zh, c + 1)
                n, lo = split_rows(c, z0h[c % 3], z0l[c % 3])
                nc.vector.tensor_tensor(lo[0:n, :], zf[c % 2][0:n, :], z0h[c % 3][0:n, :].bitcast(f32),
                                        ALU.subtract).then_inc(s_zl, 1)

            def split_h0(g, p, n=slice(0, GN)):
                dve.wait_ge(s_h0h, g + (2 if n.stop == GN else 1))
                nc.vector.scalar_tensor_tensor(out=h0l[p][:, n], in0=bankh[:, n], scalar=b0c[:, 0:1],
                                               in1=h0h[p][:, n].bitcast(f32), op0=ALU.add,
                                               op1=ALU.subtract).then_inc(s_h0l, 1)

            def fold(t, a, step):
                if step == 0:
                    dve.wait_ge(s_s, (t + 1) * NS)
                    dve.wait_ge(s_q, (t + 1) * ADDS)
                    dve.wait_ge(s_v, (t + 1) * VOPS)
                    if not (isinstance(t, int) and t == 0):
                        dve.wait_ge(s_f, t * FOLD)
                    nc.vector.tensor_reduce(h1[:, :], slots[a][:, :, :].rearrange("p c s -> p s c"),
                                            AX.X, ALU.add).then_inc(s_f, 1)
                elif step == 1:
                    dve.wait_ge(s_f, t * FOLD + 1)
                    if not (isinstance(t, int) and t == 0):
                        dve.wait_ge(s_g, t)
                    nc.vector.tensor_copy(h1h[:, :], h1[:, :]).then_inc(s_f, 1)
                else:
                    dve.wait_ge(s_f, t * FOLD + 2)
                    nc.vector.tensor_tensor(h1l[:, :], h1[:, :], h1h[:, :].bitcast(f32),
                                            ALU.subtract).then_inc(s_f, 1)

            def sum_w0(n):
                c = W0C[n]
                dve.wait_ge(s_w0in[n], 32)
                nc.vector.tensor_tensor(w0f[:, c, :], w0a[:, c, :], w0b[:, c, :], ALU.add).then_inc(s_w0, 1)

            sum_w0(0)
            for c in range(NCH):
                pairs(0, c, 0)
                if c >= 1 and c != 2:
                    split_first(c - 1)
                if c == 1:
                    sum_w0(1)
                    split_first(1)
            split_first(NCH - 1)
            for k in range(NQ):
                if k not in W1_GPSIMD:
                    dve.wait_ge(s_wh, k + 1)
                    nc.vector.tensor_tensor(wl[:, columns(k)], w1f[:, columns(k)], wh[:, columns(k)].bitcast(f32),
                                            ALU.subtract).then_inc(s_wd, 1)
                if k in H0_FIRST_AT:
                    dve.wait_ge(s_first, 48)
                    split_h0(0, 0, FIRST[H0_FIRST_AT.index(k)])
            dve.wait_ge(s_const, 16 * 4)
            for c in early(PAIRS_U):
                pairs(1, c, 1)

            def round_w2(k):
                if k >= W2E:
                    dve.wait_ge(s_t, last_quad(k))
                else:
                    dve.wait_ge(s_l0, NG * NCH)
                dve.wait_ge(s_w2in[k >= W2S], 16)
                nc.vector.tensor_copy(w2_split(k)[0], w2_staged(k)).then_inc(s_wv, 1)

            def split_g(m):
                h, i = m // F, m % F
                dve.wait_ge(s_gh, m + 1)
                nc.vector.tensor_tensor(half(gl[m % GR]), G[:, h * HG:(h + 1) * HG, i, :],
                                        half(gh[m % GR]).bitcast(f32), ALU.subtract).then_inc(s_gl, 1)

            def body(r, first, last):
                for g, p, q, t, ti in turns(r):
                    a = ti % 2
                    if q == 0:
                        dve.wait_ge(s_x[p], (r + 1) * 16)
                    for k in range(NQ):
                        u = q * NQ + k
                        if k in VQ:
                            n = VQ.index(k)
                            dve.wait_ge(s_t, g * GQ + (u + 1))
                            if n == 0:
                                dve.wait_ge(s_s, t * NS + 1)
                            for m in range(QI):
                                i = QI * k + m
                                if n:
                                    dve.wait_ge(s_v, t * VOPS + (QI * (n - 1) + m + 1))
                                part = slots[a][:, ACC + m, :]
                                nc.vector.scalar_tensor_tensor(
                                    out=part, in0=bankv[(ti * NV + n) % RING][:, m * S:(m + 1) * S],
                                    scalar=xg[p][:, q, i:i + 1],
                                    in1=part if n else prod[:, 0, m * S:(m + 1) * S],
                                    op0=ALU.mult, op1=ALU.add).then_inc(s_v, 1)
                        c, ahead = chunk_steps(PAIRS_U).get(u, (0, 0))
                        if ahead and not (last and p + ahead >= PG):
                            pairs(g + ahead, c, (p + ahead) % 2)
                        if u == H0_SPLIT_AT and not (last and p == PG - 1):
                            split_h0(g + 1, 1 - p)
                        if last and p == PG - 1 and W2_ROUND_U.get(u, 0) % 2:
                            round_w2(W2_ROUND_U[u])
                        if last and p == PG - 1 and u in G_SPLIT_U:
                            split_g(G_SPLIT_U[u])
                        if k in FOLD_AT and not (first and ti == 0):
                            fold(t - 1, 1 - a, FOLD_AT.index(k))

            bodies(dve, body)
            for h in range(2):
                for i in range(F):
                    m = h * F + i
                    if h == 0 and W2_ROUND_I.get(i, 0) % 2:
                        round_w2(W2_ROUND_I[i])
                    if m not in G_SPLIT_U.values() and not by_gpsimd(m):
                        split_g(m)
                    if h == 0 and i in LATE_FOLD:
                        fold(NT - 1, (NT - 1) % 2, LATE_FOLD.index(i))
            for bt in range(B // P):
                dve.wait_ge(s_yt, bt + 1)
                nc.vector.tensor_copy(osb[:, bt, 0:2 * S], banks[bt % 2][:, 0:2 * S]).then_inc(s_yo, 1)

        @block.gpsimd
        def _(pool):
            nc.gpsimd.memset(one[:, :], 1.0).then_inc(s_mk, 1)
            for p in range(2):
                nc.gpsimd.memset(xblk[p][:, :, :, :].bitcast(f32), 0.0).then_inc(s_mk, 1)
            for n in range(len(XB) - 1):
                load_rest(pool, 0, n, s_xr[n])
            for n, c in enumerate(W0C):
                c = slice(c.start, min(c.stop, MCH))
                pool.wait_ge(s_w0h, n + 1)
                nc.gpsimd.tensor_tensor(w0l[:, c, :], w0f[:, c, :], w0h[:, c, :].bitcast(f32),
                                        ALU.subtract).then_inc(s_w0l, 1)
                if n == 0:
                    pool.dma_start(b0c[:, :], b0).then_inc(s_first, 16)
                    pool.dma_start(msk[:, :], mask).then_inc(s_first, 16)
                    pool.dma_start(lo_rows[:, :], rows).then_inc(s_first, 16)

            c, n = MCH, len(W0C)
            pool.wait_ge(s_first, 48)
            pool.wait_ge(s_w0, n)
            nc.gpsimd.tensor_tensor(w0h[:, c, :], w0f[:, c, :], lo_rows[:, 0:1].broadcast_to([P, S]),
                                    ALU.mult).then_inc(s_w0l, 1)
            pool.wait_ge(s_w0l, n + 1)
            nc.gpsimd.tensor_tensor(w0l[:, c, :], w0f[:, c, :], w0h[:, c, :].bitcast(f32),
                                    ALU.subtract).then_inc(s_w0l, 1)
            for k in W1_GPSIMD:
                pool.wait_ge(s_wh, k + 1)
                nc.gpsimd.tensor_tensor(wl[:, columns(k)], w1f[:, columns(k)], wh[:, columns(k)].bitcast(f32),
                                        ALU.subtract).then_inc(s_wl, 1)
            pool.wait_ge(s_mk, 3)
            for p in range(2):
                nc.gpsimd.tensor_copy(xblk[p][:, 0, F, :], msk[:, :]).then_inc(s_mk, 1)

            def split_pairs(g, c, p):
                e = (p + c) % 2
                pool.wait_ge(s_zh, g * NCH + (c + 1))
                n, lo = split_rows(c, zh[e], zl[e])
                nc.gpsimd.tensor_tensor(lo[0:n, :], zf[e][0:n, :], zh[e][0:n, :].bitcast(f32),
                                        ALU.subtract).then_inc(s_zl, 1)

            for c in early(SPLIT_U):
                split_pairs(1, c, 1)

            def split_w2(k):
                if k % 2:
                    pool.wait_ge(s_wv, k // 2 + 1)
                else:
                    pool.wait_ge(s_wh, NQ + k // 2 + 1)
                rounded, rest = w2_split(k)
                nc.gpsimd.tensor_tensor(rest, w2_staged(k), rounded.bitcast(f32), ALU.subtract).then_inc(s_wl, 1)

            def body(r, first, last):
                for g, p, q, t, ti in turns(r):
                    a = ti % 2
                    sums = slots[a][:, SUM:SUM + QI, :].rearrange("p c s -> p (c s)")
                    if q == 0:
                        pool.wait_ge(s_x[p], (r + 1) * 16)
                        nc.gpsimd.tensor_tensor(xs[p][:, :, 0, :].bitcast(f32r), xg[p][:, :, :],
                                                one[:, :].unsqueeze(2).broadcast_to([P, TG, F]),
                                                ALU.mult).then_inc(s_xs, 1)
                        pool.wait_ge(s_xs, 2 * g + 1)
                        nc.gpsimd.tensor_tensor(xs[p][:, :, 1, :], xg[p][:, :, :], xs[p][:, :, 0, :],
                                                ALU.subtract).then_inc(s_xs, 1)
                        pool.wait_ge(s_xs, 2 * g + 2)
                    for k in range(NQ):
                        u = q * NQ + k
                        if k in SUM_AT:
                            n = SUM_AT.index(k) + 2
                            pool.wait_ge(s_s, t * NS + (n + 1))
                            if n == 2:
                                if not (first and ti < 2):
                                    pool.wait_ge(s_f, t * FOLD + (1 - 2 * FOLD))
                                nc.gpsimd.tensor_tensor(sums, prod[:, 1, :], prod[:, 2, :],
                                                        ALU.add).then_inc(s_q, 1)
                            else:
                                pool.wait_ge(s_q, t * ADDS + (n - 2))
                                nc.gpsimd.tensor_tensor(sums, sums, prod[:, n, :], ALU.add).then_inc(s_q, 1)
                        c, ahead = chunk_steps(SPLIT_U).get(u, (0, 0))
                        if ahead and not (last and p + ahead >= PG):
                            split_pairs(g + ahead, c, (p + ahead) % 2)
                        if last and p == PG - 1 and u in W2_SPLIT_U:
                            split_w2(W2_SPLIT_U[u])
                        if k == BLOCKS_AT:
                            if first and ti < 2:
                                pool.wait_ge(s_mk, 5)
                            else:
                                pool.wait_ge(s_g, t - 1)
                            nc.gpsimd.tensor_tensor(
                                xblk[a][:, :, 0:F, :], xs[p][:, q, :, :].unsqueeze(3).broadcast_to([P, 2, F, BT]),
                                msk[:, :].unsqueeze(1).unsqueeze(1).broadcast_to([P, 2, F, BT]),
                                ALU.mult).then_inc(s_xk, 1)

            bodies(pool, body)
            for k in range(W2N):
                if k not in W2_SPLIT_U.values():
                    split_w2(k)
            for m in range(2 * F):
                h, i = m // F, m % F
                if by_gpsimd(m):
                    pool.wait_ge(s_gh, m + 1)
                    nc.gpsimd.tensor_tensor(half(gl[m % GR]), G[:, h * HG:(h + 1) * HG, i, :],
                                            half(gh[m % GR]).bitcast(f32), ALU.subtract).then_inc(s_gp, 1)

        @block.tensor
        def _(pe):
            def product(o, ah, al, bh, bl, start=True, stop=True):
                nc.tensor.matmul(o, ah, bh, start=start, stop=False)
                nc.tensor.matmul(o, ah, bl, start=False, stop=False)
                return nc.tensor.matmul(o, al, bh, start=False, stop=stop)

            def layer0(g, c, p):
                n, e = ROWS[c], (p + c) % 2
                hi, lo = (z0h[c % 3], z0l[c % 3]) if isinstance(g, int) and g == 0 else (zh[e], zl[e])
                pe.wait_ge(s_zl, g * NCH + (c + 1))
                if c < MCH:
                    product(bankh[:, :], w0h[0:n, c, :], w0l[0:n, c, :], hi[0:n, :], lo[0:n, :],
                            start=(c == 0), stop=False).then_inc(s_l0, 1)
                else:
                    nc.tensor.matmul(bankh[:, :], w0l[0:n, c, :], hi[0:n, :], start=False,
                                     stop=True).then_inc(s_l0, 1)

            def into_g(t, a):
                pe.wait_ge(s_f, (t + 1) * FOLD)
                pe.wait_ge(s_xk, t + 1)
                if not (isinstance(t, int) and t == 0):
                    pe.wait_ge(s_ge, t)
                product(bankg[:, 0:GC * BT], h1h[:, :], h1l[:, :],
                        xblk[a][:, 0, :, :].rearrange("p c b -> p (c b)"),
                        xblk[a][:, 1, :, :].rearrange("p c b -> p (c b)")).then_inc(s_g, 1)

            for c in range(NCH):
                for n, part in enumerate(W0C):
                    if c == part.start:
                        pe.wait_ge(s_w0l, n + 1)
                if c == MCH:
                    pe.wait_ge(s_w0l, len(W0C) + 2)
                layer0(0, c, 0)

            def body(r, first, last):
                for g, p, q, t, ti in turns(r):
                    for k in range(NQ):
                        u = q * NQ + k
                        if u == 0:
                            pe.wait_ge(s_h0l, 1 if first and p == 0 else g + 2)
                        if first and ti == 1 and k == 0:
                            pe.wait_ge(s_h0l, 2)
                        if first and ti == 0:
                            if k in W1_GPSIMD:
                                pe.wait_ge(s_wl, W1_GPSIMD.index(k) + 1)
                            else:
                                pe.wait_ge(s_wd, sum(n not in W1_GPSIMD for n in range(k + 1)))
                        if k in VQ:
                            index = ti * NV + VQ.index(k)
                            before = last_use(index, RING, VBODY)
                            if not (first and before < 0):
                                pe.wait_ge(s_v, t * VOPS + QI * (before + 1 - ti * NV))
                            bank = bankv[index % RING]
                        else:
                            index = ti * NS + SQ.index(k)
                            before = last_use(index, RING, SBODY)
                            if not (first and before < 0):
                                pe.wait_ge(s_s, t * NS + (before + 1 - ti * NS))
                            bank = banks[index % RING]
                        columns_q = slice(q * P, (q + 1) * P)
                        product(bank[:, 0:S * WIDE[k]], h0h[p][:, columns_q], h0l[p][:, columns_q],
                                wh[:, columns(k)], wl[:, columns(k)]).then_inc(s_t, 1)
                        c, ahead = chunk_steps(LAYER0_U).get(u, (0, 0))
                        if ahead and not (last and p + ahead >= PG):
                            if c == 0:
                                pe.wait_ge(s_h0l, g + 2)
                            layer0(g + ahead, c, (p + ahead) % 2)
                        if k == INTO_G_AT and not (first and ti < 2):
                            into_g(t - 2, ti % 2)

            bodies(pe, body)
            for h in range(2):
                pe.wait_ge(s_v, NT * VOPS + QI * (last_use(h + VBODY, RING, VBODY) + 1 - VBODY))
                for i in range(F):
                    m = h * F + i
                    part = sum(i >= start for start in W2P) - 1
                    if h == 0 and i == W2P[part]:
                        pe.wait_ge(s_wl, len(W1_GPSIMD) + part + 1)
                    if by_gpsimd(m):
                        pe.wait_ge(s_gp, earlier_by_gpsimd(m) + 1)
                    else:
                        pe.wait_ge(s_gl, m - earlier_by_gpsimd(m) + 1)
                    rounded, rest = (w[:, (i - W2P[part]) * S:(i - W2P[part] + 1) * S] for w in w2_split(part))
                    product(banky[h][:, 0:HB], rounded, rest,
                            gh[m % GR], gl[m % GR], start=(i == 0), stop=(i == F - 1)).then_inc(s_gu, 1)
                    if h == 0 and i in LATE:
                        t = NT - 2 + LATE.index(i)
                        into_g(t, t % 2)
            for bt in range(B // P):
                if bt == 0:
                    pe.wait_ge(s_yc, 2)
                if bt * P == HB:
                    pe.wait_ge(s_yc, 3)
                if bt >= 2:
                    pe.wait_ge(s_yo, bt - 1)
                nc.tensor.transpose(banks[bt % 2][:, 0:S], y1s[:, bt * P:(bt + 1) * P], idn[:, :])
                nc.tensor.transpose(banks[bt % 2][:, S:2 * S], y2s[:, bt * P:(bt + 1) * P],
                                    idn[:, :]).then_inc(s_yt, 1)


def kernel(r_x, L0_rec_w0, L0_rec_b0, L0_rec_w1, L0_rec_b1, L0_rec_w2, L0_rec_b2):
    import numpy as np
    import concourse.bacc as bacc
    from concourse.bass_utils import run_bass_kernel_spmd

    x = np.asarray(r_x)
    xt = x.transpose(1, 0, 2).reshape(F, N)
    w0 = np.asarray(L0_rec_w0).reshape(F, F, S)
    w0p = np.zeros((P, NCH, S), w0.dtype)
    w0q = np.zeros((P, NCH, S), w0.dtype)
    i = np.arange(F)
    for k in range(X0):
        c, r = divmod(k, SC)
        w0p[r * F:(r + 1) * F, c] = w0[i, (i + k) % F]
        if k:
            w0q[r * F:(r + 1) * F, c] = w0[(i + k) % F, i]
    for n in range(KX):
        k = X0 + n
        last = np.arange(TOP, min(TOP + REST, F - k))
        w0p[R:P, n], w0q[R:P, n] = w0[i[:TOP], i[:TOP] + k], w0[i[:TOP] + k, i[:TOP]]
        for copy in range(3):
            rows = copy * LR + n * REST + last - TOP
            w0p[rows, MCH], w0q[rows, MCH] = w0[last, last + k], w0[last + k, last]
    arrays = {
        "xt2": np.concatenate([xt, xt[:X0]], axis=0),
        "xn": x.reshape(NT, BT, F, D).transpose(1, 3, 0, 2).reshape(P, NT, F),
        "w0p": w0p,
        "w0q": w0q,
        "w1": np.asarray(L0_rec_w1).reshape(F, S, S).transpose(1, 0, 2).reshape(S, F * S),
        "w2": np.asarray(L0_rec_w2).reshape(F, S, S).transpose(1, 0, 2).reshape(S, F * S),
        "b0": np.asarray(L0_rec_b0).reshape(S, 1),
        "b1": np.asarray(L0_rec_b1).reshape(S),
        "b2": np.asarray(L0_rec_b2).reshape(S, 1),
        "mask": np.kron(np.eye(BT, dtype=np.float32), np.ones((D, 1), np.float32)),
        "rows": (np.arange(P).reshape(P, 1) >= 2 * LR).astype(np.float32),
        "ident": np.eye(P, dtype=np.float32),
    }
    nc = bacc.Bacc("TRN2", target_bir_lowering=False, num_devices=1)
    ins, args = {}, []
    for name, a in arrays.items():
        ins[f"in_{name}"] = np.ascontiguousarray(a)
        args.append(nc.dram_tensor(f"in_{name}", a.shape, mybir.dt.from_np(a.dtype), kind="ExternalInput").ap())
    args.append(nc.dram_tensor("out_y", (B, 2 * S), mybir.dt.float32, kind="ExternalOutput").ap())
    build(nc, *args)
    r = run_bass_kernel_spmd(nc, [ins], core_ids=[0])
    return r.results[0]["out_y"]
```
